# Optimizing a Trainium2 kernel written in Bass

```python
import numpy as np
import jax
import jax.numpy as jnp

def _softmax(x, axis=-1):
    return jax.nn.softmax(x, axis=axis)

def _gelu(x):
    return jax.nn.gelu(x, approximate=True)

def _silu(x):
    return jax.nn.silu(x)

def _sigmoid(x):
    return jax.nn.sigmoid(x)

def _layernorm(x, axis=-1, eps=1e-05):
    m = jnp.mean(x, axis=axis, keepdims=True)
    v = jnp.var(x, axis=axis, keepdims=True)
    return (x - m) / jnp.sqrt(v + eps)

def _scatter_add(tgt, idx, src, axis=0):
    return tgt.at[idx].add(src)

def _segment_sum(src, seg, n):
    return jax.ops.segment_sum(src, seg, n)
kernel_name = 'mk_prb_d1_jaxref_r8_bee50d'

def setup_inputs(seed: int=0):
    np.random.seed(seed)
    _w = jnp.asarray

    def _L0_attn_setup():
        import jax, jax.numpy as jnp
        import numpy as np
        import math
        D = 128
        H = 16
        DH = D // H

        def sinusoidal_pe(length, d):
            pos = jnp.arange(length, dtype=jnp.float32)[:, None]
            div = jnp.exp(jnp.arange(0, d, 2, dtype=jnp.float32) * (-math.log(10000.0) / d))
            ang = pos * div
            return jnp.stack([jnp.sin(ang), jnp.cos(ang)], axis=-1).reshape(length, d)

        def _relative_shift(pos_score):
            B, Hh, S1, S2 = pos_score.shape
            padded = jnp.concatenate([jnp.zeros((B, Hh, S1, 1), pos_score.dtype), pos_score], axis=-1)
            padded = padded.reshape(B, Hh, S2 + 1, S1)
            return padded[:, :, 1:].reshape(B, Hh, S1, S2)
        key = jax.random.key(seed)
        ks = jax.random.split(key, 12)
        s = 0.02
        x = jax.random.normal(ks[0], (2, 256, D), dtype=jnp.float32)
        return {'x': x, 'ln_g': jnp.ones((D,), jnp.float32), 'ln_b': jnp.zeros((D,), jnp.float32), 'Wq': jax.random.normal(ks[1], (D, D), jnp.float32) * s, 'bq': jnp.zeros((D,), jnp.float32), 'Wk': jax.random.normal(ks[2], (D, D), jnp.float32) * s, 'bk': jnp.zeros((D,), jnp.float32), 'Wv': jax.random.normal(ks[3], (D, D), jnp.float32) * s, 'bv': jnp.zeros((D,), jnp.float32), 'Wp': jax.random.normal(ks[4], (D, D), jnp.float32) * s, 'Wo': jax.random.normal(ks[5], (D, D), jnp.float32) * s, 'bo': jnp.zeros((D,), jnp.float32), 'u_bias': jax.random.normal(ks[6], (H, DH), jnp.float32) * 0.05, 'v_bias': jax.random.normal(ks[7], (H, DH), jnp.float32) * 0.05}
    _L0_attn_in = _L0_attn_setup()

    def _L0_ffn_setup():
        import jax, jax.numpy as jnp
        import numpy as np
        import math
        D_IN = 128
        FEATURES = (512, 512, 128)
        BATCH, SEQ = (8, 256)

        def _conn_dense(kernel_bool, x):
            w = jnp.where(kernel_bool, jnp.float32(1.0), jnp.float32(-1.0))
            return x @ w
        key = jax.random.key(seed)
        kx, kk0, kk1, kk2 = jax.random.split(key, 4)
        x = jax.random.normal(kx, (BATCH, SEQ, D_IN), dtype=jnp.float32)
        k0 = jax.random.randint(kk0, (2 * D_IN, FEATURES[0]), 0, 2).astype(jnp.bool_)
        k1 = jax.random.randint(kk1, (FEATURES[0], FEATURES[1]), 0, 2).astype(jnp.bool_)
        k2 = jax.random.randint(kk2, (FEATURES[1], FEATURES[2]), 0, 2).astype(jnp.bool_)
        s0 = jnp.asarray(1.0 / math.sqrt(2 * D_IN), dtype=jnp.float32)
        s1 = jnp.asarray(1.0 / math.sqrt(FEATURES[0]), dtype=jnp.float32)
        s2 = jnp.asarray(1.0 / math.sqrt(FEATURES[1]), dtype=jnp.float32)
        return {'x': x, 'k0': k0, 'k1': k1, 'k2': k2, 's0': s0, 's1': s1, 's2': s2}
    _L0_ffn_in = _L0_ffn_setup()
    _d = {'L0_attn_x': _L0_attn_in['x'], 'L0_attn_ln_g': _L0_attn_in['ln_g'], 'L0_attn_ln_b': _L0_attn_in['ln_b'], 'L0_attn_Wq': _L0_attn_in['Wq'], 'L0_attn_bq': _L0_attn_in['bq'], 'L0_attn_Wk': _L0_attn_in['Wk'], 'L0_attn_bk': _L0_attn_in['bk'], 'L0_attn_Wv': _L0_attn_in['Wv'], 'L0_attn_bv': _L0_attn_in['bv'], 'L0_attn_Wp': _L0_attn_in['Wp'], 'L0_attn_Wo': _L0_attn_in['Wo'], 'L0_attn_bo': _L0_attn_in['bo'], 'L0_attn_u_bias': _L0_attn_in['u_bias'], 'L0_attn_v_bias': _L0_attn_in['v_bias'], 'L0_ffn_k0': _L0_ffn_in['k0'], 'L0_ffn_k1': _L0_ffn_in['k1'], 'L0_ffn_k2': _L0_ffn_in['k2'], 'L0_ffn_s0': _L0_ffn_in['s0'], 'L0_ffn_s1': _L0_ffn_in['s1'], 'L0_ffn_s2': _L0_ffn_in['s2']}
    _x0 = _d['L0_attn_x']
    _d['L0_attn_x'] = jax.random.normal(jax.random.fold_in(jax.random.key(seed), 1), (16, 512, 128), dtype=_x0.dtype)
    del _x0
    return _d

def reference(L0_attn_x, L0_attn_ln_g, L0_attn_ln_b, L0_attn_Wq, L0_attn_bq, L0_attn_Wk, L0_attn_bk, L0_attn_Wv, L0_attn_bv, L0_attn_Wp, L0_attn_Wo, L0_attn_bo, L0_attn_u_bias, L0_attn_v_bias, L0_ffn_k0, L0_ffn_k1, L0_ffn_k2, L0_ffn_s0, L0_ffn_s1, L0_ffn_s2):

    def _L0_attn_ref(x, ln_g, ln_b, Wq, bq, Wk, bk, Wv, bv, Wp, Wo, bo, u_bias, v_bias):
        import jax, jax.numpy as jnp
        import numpy as np
        import math
        D = 128
        H = 16
        DH = D // H

        def sinusoidal_pe(length, d):
            pos = jnp.arange(length, dtype=jnp.float32)[:, None]
            div = jnp.exp(jnp.arange(0, d, 2, dtype=jnp.float32) * (-math.log(10000.0) / d))
            ang = pos * div
            return jnp.stack([jnp.sin(ang), jnp.cos(ang)], axis=-1).reshape(length, d)

        def _relative_shift(pos_score):
            B, Hh, S1, S2 = pos_score.shape
            padded = jnp.concatenate([jnp.zeros((B, Hh, S1, 1), pos_score.dtype), pos_score], axis=-1)
            padded = padded.reshape(B, Hh, S2 + 1, S1)
            return padded[:, :, 1:].reshape(B, Hh, S1, S2)
        B, S, Dm = x.shape
        dh = Dm // H
        scale = dh ** (-0.5)
        pe = sinusoidal_pe(S, Dm)
        mu = jnp.mean(x, axis=-1, keepdims=True)
        var = jnp.var(x, axis=-1, keepdims=True)
        xn = (x - mu) / jnp.sqrt(var + 1e-05) * ln_g + ln_b
        q = (xn @ Wq + bq).reshape(B, S, H, dh)
        k = (xn @ Wk + bk).reshape(B, S, H, dh)
        v = (xn @ Wv + bv).reshape(B, S, H, dh)
        p = (pe @ Wp).reshape(S, H, dh)
        content = jnp.einsum('bihd,bjhd->bhij', q + u_bias, k)
        pos = jnp.einsum('bihd,jhd->bhij', q + v_bias, p)
        pos = _relative_shift(pos)
        attn = jax.nn.softmax((content + pos) * scale, axis=-1)
        head = jnp.einsum('bhij,bjhd->bihd', attn, v).reshape(B, S, Dm)
        return head @ Wo + bo

    def _L0_ffn_ref(x, k0, k1, k2, s0, s1, s2):
        import jax, jax.numpy as jnp
        import numpy as np
        import math
        D_IN = 128
        FEATURES = (512, 512, 128)
        BATCH, SEQ = (8, 256)

        def _conn_dense(kernel_bool, x):
            w = jnp.where(kernel_bool, jnp.float32(1.0), jnp.float32(-1.0))
            return x @ w
        h = jnp.concatenate([x, -x], axis=-1)
        h = s0 * _conn_dense(k0, h)
        h = jax.nn.relu(h) * 2
        h = s1 * _conn_dense(k1, h)
        h = jax.nn.relu(h) * 2
        h = s2 * _conn_dense(k2, h)
        return h
    x = L0_attn_x
    xn = _layernorm(x, axis=-1)
    x = x + _L0_attn_ref(xn, L0_attn_ln_g, L0_attn_ln_b, L0_attn_Wq, L0_attn_bq, L0_attn_Wk, L0_attn_bk, L0_attn_Wv, L0_attn_bv, L0_attn_Wp, L0_attn_Wo, L0_attn_bo, L0_attn_u_bias, L0_attn_v_bias) + _L0_ffn_ref(xn, L0_ffn_k0, L0_ffn_k1, L0_ffn_k2, L0_ffn_s0, L0_ffn_s1, L0_ffn_s2)
    return x

_drawn_inputs = setup_inputs


def setup_inputs(seed=0):
    import zlib

    import numpy as np

    out = dict(_drawn_inputs(seed))
    spreads = {'L0_attn_ln_g': (1.0, 0.6),
     'L0_attn_ln_b': (0.0, 0.8),
     'L0_attn_bq': (0.0, 0.8),
     'L0_attn_bk': (0.0, 2.0),
     'L0_attn_bv': (0.0, 0.8),
     'L0_attn_bo': (0.0, 0.333)}
    factors = {'L0_attn_Wq': 8.0,
     'L0_attn_Wk': 8.0,
     'L0_attn_Wv': 8.0,
     'L0_attn_Wp': 8.0,
     'L0_attn_Wo': 5.584,
     'L0_attn_u_bias': 8.0,
     'L0_attn_v_bias': 8.0}
    for name, (base, spread) in spreads.items():
        noise = np.random.default_rng([zlib.crc32(name.encode()), seed]).standard_normal(out[name].shape)
        drawn = base * np.exp(spread * noise) if base else spread * noise
        out[name] = jnp.asarray(drawn.astype(out[name].dtype))
    for name, factor in factors.items():
        out[name] = (out[name] * factor).astype(out[name].dtype)
    return out
```

```python
from contextlib import ExitStack

import concourse.bass as bass
from concourse import mybir

ALU = mybir.AluOpType
ACT = mybir.ActivationFunctionType
F32 = mybir.dt.float32
BF16 = mybir.dt.bfloat16
U8 = mybir.dt.uint8

P = 128
EPS = 1e-5
Q_PIECES = (0, 0, 0, 1, 1, 2)
K_PIECES = (2, 0, 1, 0, 1, 0)
NR = len(Q_PIECES)


def attention_mlp(nc, x, ln_g, ln_b, wq, bq, wk, bk, wv, bv, wp, wo, bo, u_bias, v_bias,
                  k0, k1, k2, s0, s1, s2, pe_t, ident, out):
    B, S, D = x.shape
    H, DH = 16, 8
    assert D == P and H * DH == P and S == 512 and k0.shape[1] == S
    NT = S // P
    UNITS = B * H
    PAIRS = H // 2
    KR = NR * DH
    HALF = PAIRS // 2
    F1, F2 = k0.shape[1], k1.shape[1]
    C1, C2 = F1 // P, F2 // P
    SCALE = float(DH) ** -0.5
    PITCH = S + 1

    CONTENT_LAG = 4
    TURN_LAG = CONTENT_LAG + 1
    N_POS = 3
    N_SC = 5
    N_SHIFT = 4
    N_PT = 3

    shift = nc.dram_tensor("shift", [N_SHIFT, S * PITCH], F32, kind="Internal").ap()
    stk = [nc.dram_tensor(f"stk_{n}", [2, NR, DH * PAIRS, S], BF16, kind="Internal").ap()
           for n in ("qu", "qv", "k", "p")]
    heads_d = nc.dram_tensor("heads_d", [P, NT, P], F32, kind="Internal").ap()
    sums_d = nc.dram_tensor("sums_d", [P, NT, P], F32, kind="Internal").ap()

    with ExitStack() as ctx:
        def sb(name, shape, dt=F32):
            return ctx.enter_context(nc.sbuf_tensor(name, shape, dt))

        def psum(name, shape):
            return ctx.enter_context(nc.psum_tensor(name, shape, F32))

        def sem(name):
            return ctx.enter_context(nc.semaphore(name))

        id_sb = sb("id_sb", [P, P])
        w_sb = {n: sb(f"w_{n}", [P, D]) for n in ("q", "k", "v", "p", "o")}
        cols = sb("cols", [P, 10])
        G, BB, BQ, BK, UB, VB, S0, S1, S2 = (cols[:, i:i + 1] for i in range(9))
        col2 = sb("col2", [P, 4])
        bv_row = sb("bv_row", [P, D])
        bo_row = sb("bo_row", [P, D])
        k0_u8 = sb("k0_u8", [P, 2, F1], U8)
        k1_u8 = sb("k1_u8", [P, C1, F2], U8)
        k2_u8 = sb("k2_u8", [P, C2, D], U8)
        w0 = sb("w0", [P, F1])
        w1 = sb("w1", [P, C1, F2])
        w2 = sb("w2", [P, C2, D])
        half_pow = sb("half_pow", [P, NT])

        x_sb = sb("x_sb", [P, 2, NT, D])
        xb_sb = sb("xb_sb", [P, 3, NT, D])
        x1_sb = sb("x1_sb", [P, NT, D])
        z_sb = sb("z_sb", [P, NT, D])
        stats = sb("stats", [P, 2, NT, 6])
        mv = sb("mv", [P, 2, NT, 2])
        var_eps = sb("var_eps", [P, 2, NT])
        rstd = sb("rstd", [P, 2, NT])
        x1_t = sb("x1_t", [P, 2, NT, P])
        z_t = sb("z_t", [P, S])
        full = [sb(f"full_{n}", [P, S]) for n in ("qu", "qv", "k")]
        pe_sb = full[1]
        rest = sb("rest", [P, S])
        piece = [[sb(f"piece_{n}{i}", [P, S], BF16) for i in range(3)] for n in ("qu", "qv", "k")]
        stack = [sb(f"stack_{n}", [P, PAIRS, S], BF16) for n in ("qu", "qv", "k", "p")]
        QU, QV, KK, PP = stack
        v_sb = sb("v_sb", [P, 2, NT, H, 2 * DH])

        pos_sb = sb("pos_sb", [P, N_POS, NT, PITCH])
        sc_sb = sb("sc_sb", [P, N_SC, NT, S])
        nmax = sb("nmax", [P, N_SC, NT])
        pt_sb = sb("pt_sb", [P, N_PT, 2, S])
        o_sb = sb("o_sb", [P, H, P])
        o_t = sb("o_t", [P, S])
        l_t = sb("l_t", [P, S])

        h1 = sb("h1", [P, C1, S])
        h2 = sb("h2", [P, C2, S])
        y_sb = sb("y_sb", [P, 2, NT, D])
        out_sb = sb("out_sb", [P, NT, D])

        ps_pos = psum("ps_pos", [P, 2, S])
        ps_con = psum("ps_con", [P, 2, S])
        ps_pt = psum("ps_pt", [P, 2, S])
        ps_av = psum("ps_av", [P, 4, P])
        ps_job = psum("ps_job", [P, S])

        s_w = sem("s_w")
        s_ones = sem("s_ones")
        s_wf = sem("s_wf")
        s_x = [sem("s_x0"), sem("s_x1")]
        s_chain = sem("s_chain")
        s_pool = sem("s_pool")
        s_st1, s_st2 = sem("s_st1"), sem("s_st2")
        s_x1, s_z = sem("s_x1n"), sem("s_z")
        s_job = sem("s_job")
        s_jev = sem("s_jev")
        s_split = [sem(f"s_split{i}") for i in range(3)]
        s_pw = [sem(f"s_pw{i}") for i in range(3)]
        s_stk = [[sem(f"s_stk{i}{j}") for j in range(2)] for i in range(4)]
        s_pos, s_con, s_pt, s_av = sem("s_pos"), sem("s_con"), sem("s_pt"), sem("s_av")
        s_pa, s_pd = sem("s_pa"), sem("s_pd")
        s_out_w = [sem(f"s_pout{i}") for i in range(N_POS)]
        s_in = [sem(f"s_in{i}") for i in range(N_SC)]
        s_ttr, s_exp = sem("s_ttr"), sem("s_exp")
        s_ta, s_td = sem("s_ta"), sem("s_td")
        s_oev = sem("s_oev")
        s_hw, s_hr = sem("s_hw"), sem("s_hr")
        s_on = sem("s_on")
        s_out = sem("s_out")

        def wait(eng, s, n):
            if n > 0:
                eng.wait_ge(s, n)

        SLOT = {}
        order = []

        def add(step, name, b, c=0):
            SLOT.setdefault(step, []).append((name, b, c))

        for it in range(-1, B + 1):
            at = 16 * it
            if it == -1:
                add(at, "P", 0)
            if it + 1 < B:
                for i, n in enumerate(("T1", "TZ", "Q", "K")):
                    add(at + i, n, it + 1)
            if 0 <= it < B:
                for c in range(C1):
                    add(at + 4 + c, "L0", it, c)
                for c in range(C2):
                    add(at + 8 + c, "L1", it, c)
                add(at + 12, "L2", it)
            if it + 1 < B:
                add(at + 13, "V", it + 1)
            if it >= 1:
                add(at + 14, "WO", it - 1)
        STEPS = range(-16, 16 * B + 16)
        for n in STEPS:
            order += SLOT.get(n, [])
        JOB = {j: i + 1 for i, j in enumerate(order)}

        def jobs(n):
            return SLOT.get(n, [])

        def job(name, b, c=0):
            return JOB[(name, b, c)] if b >= 0 else 0

        def unit(n, lag):
            return n - lag if 0 <= n - lag < UNITS else None

        block = ctx.enter_context(nc.Block())

        @block.sync
        def _(sp):
            def load_x(b):
                wait(sp, s_x1, b - 1)
                sp.dma_start(x_sb[:, b % 2], x[b].rearrange("(p t) d -> p t d", t=NT)) \
                  .then_inc(s_x[b % 2], 16)

            def row(v, n):
                return bass.AP(tensor=v.tensor, offset=0, ap=[[0, P], [1, n]])

            load_x(0)
            small = [(id_sb[:, :], ident), (w_sb["p"][:, :], wp), (pe_sb[:, :], pe_t),
                     (w_sb["q"][:, :], wq), (w_sb["k"][:, :], wk), (w_sb["v"][:, :], wv),
                     (w_sb["o"][:, :], wo)]
            small += [(cols[:, i:i + 1], v.rearrange("(p a) -> p a", a=1))
                      for i, v in enumerate((ln_g, ln_b, bq, bk, u_bias, v_bias))]
            small += [(cols[:, 6 + i:7 + i], row(v, 1)) for i, v in enumerate((s0, s1, s2))]
            small += [(bv_row[:, :], row(bv, D)), (bo_row[:, :], row(bo, D)),
                      (k0_u8[:, :, :], k0.rearrange("(a p) n -> p a n", p=P)),
                      (k1_u8[:, :, :], k1.rearrange("(a p) n -> p a n", p=P)),
                      (k2_u8[:, :, :], k2.rearrange("(a p) n -> p a n", p=P))]
            assert len(small) == N_SMALL
            for dst, src in small:
                sp.dma_start(dst, src).then_inc(s_w, 16)
            load_x(1)

            def write_pieces(i, rounds, which, dst):
                wait(sp, s_split[i], rounds)
                for n in range(3):
                    at = [r for r in range(NR) if which[r] == n]
                    step = at[1] - at[0] if len(at) > 1 else 1
                    for par in range(2):
                        d = dst[par, at[0]:at[-1] + 1:step].rearrange("r q c -> q r c")
                        s = piece[i][n][64 * par:64 * par + 64, :].unsqueeze(1) \
                            .broadcast_to([64, len(at), S])
                        sp.dma_start(d, s).then_inc(s_pw[i], 16)

            def read_stack(i, j, rounds_w, half):
                wait(sp, s_pw[i], 96 * rounds_w)
                for par in range(2):
                    src = stk[j][par].rearrange("r (d q) c -> (r d) q c", q=PAIRS)
                    q = slice(HALF * half, HALF * half + HALF)
                    sp.dma_start(stack[j][64 * par:64 * par + KR, q, :], src[:, q, :]) \
                      .then_inc(s_stk[j][half], 16)

            for n in STEPS:
                it, slot = n // 16, n % 16
                if it == -1 and slot == 1:
                    write_pieces(0, 1, K_PIECES, stk[3])
                    read_stack(0, 3, 1, 0)
                    read_stack(0, 3, 1, 1)
                if it >= 2 and slot == 1:
                    wait(sp, s_jev, job("WO", it - 2))
                    sp.dma_start(out[it - 2].rearrange("(p t) d -> p t d", t=NT),
                                 out_sb[:, :, :]).then_inc(s_out, 16)
                if 0 <= it < B and slot == CONTENT_LAG:
                    wait(sp, s_con, 4 * 16 * it)
                    for i in range(3):
                        read_stack(i, i, it + 1 + (i == 0), 1)
                if it + 1 < B and slot == 7:
                    for i, w in ((1, Q_PIECES), (2, K_PIECES), (0, Q_PIECES)):
                        if it >= 0:
                            for half in range(2):
                                sp.wait_ge(s_stk[i][half], 32 * (it + 1))
                        write_pieces(i, it + 2 + (i == 0), w, stk[i])
                if it + 1 < B and slot == CONTENT_LAG + 8:
                    wait(sp, s_con, 4 * (16 * it + 8))
                    for i in range(3):
                        read_stack(i, i, it + 2 + (i == 0), 0)
                if it >= 1 and slot == TURN_LAG + 2:
                    sp.wait_ge(s_oev, 4 * it)
                    for part, dst in enumerate((heads_d, sums_d)):
                        for t in range(NT):
                            rows = slice(32 * t + DH * part, 32 * t + DH * part + DH)
                            sp.dma_start(dst[:, t, :].rearrange("(h d) c -> d h c", d=DH), o_sb[rows, :, :]) \
                              .then_inc(s_hw, 16)
                if it >= 1 and slot == TURN_LAG + 3:
                    sp.wait_ge(s_hw, 16 * 2 * NT * it)
                    wait(sp, s_job, job("WO", it - 2))
                    sp.dma_start(o_t[:, :], heads_d.rearrange("p t c -> p (t c)")).then_inc(s_hr, 16)
                    sp.dma_start(l_t[:, :], sums_d.rearrange("p t c -> p (t c)")).then_inc(s_hr, 16)
                if it + 3 < B and slot == 13:
                    load_x(it + 3)
                u = unit(n, 1)
                if u is not None:
                    sp.wait_ge(s_out_w[u % N_POS], 16 * (u // N_POS + 1))
                    wait(sp, s_pt, 2 * (u - N_SC + 1))
                    sp.dma_start(sc_sb[:, u % N_SC].rearrange("p t c -> p (t c)"),
                                 shift[u % N_SHIFT, S - 1:S - 1 + S * S].rearrange("(p c) -> p c", p=P)) \
                      .then_inc(s_in[u % N_SC], 16)
                u = unit(n, 0)
                if u is not None:
                    sp.wait_ge(s_pa, u + 1)
                    sp.wait_ge(s_pd, u + 1)
                    if u >= N_SHIFT:
                        v = u - N_SHIFT
                        sp.wait_ge(s_in[v % N_SC], 16 * (v // N_SC + 1))
                    sp.dma_start(shift[u % N_SHIFT].rearrange("(p c) -> p c", p=P),
                                 pos_sb[:, u % N_POS].rearrange("p t c -> p (t c)")) \
                      .then_inc(s_out_w[u % N_POS], 16)
            wait(sp, s_jev, job("WO", B - 1))
            if B >= 1:
                sp.dma_start(out[B - 1].rearrange("(p t) d -> p t d", t=NT), out_sb[:, :, :]) \
                  .then_inc(s_out, 16)
            sp.wait_ge(s_out, 16 * B)

        @block.gpsimd
        def _(pool):
            done = [0]

            def own(ins):
                done[0] += 1
                ins.then_inc(s_pool, 1)
                pool.wait_ge(s_pool, done[0])

            pool.memset(half_pow[:, :], -0.5).then_inc(s_ones, 1)
            pool.memset(pos_sb[:, :, :, S:PITCH], 0.0).then_inc(s_ones, 1)
            pool.memset(v_sb[:, :, :, :, DH:2 * DH], 1.0).then_inc(s_ones, 1)
            pool.wait_ge(s_ones, 3)

            def inv_std():
                own(pool.tensor_scalar(var_eps[:, 0, :], mv[:, 0, :, 1], EPS, None, ALU.add))
                own(pool.tensor_tensor(rstd[:, 0, :], var_eps[:, 0, :], half_pow[:, :], ALU.pow))

            def inv_std2():
                own(pool.tensor_scalar(var_eps[:, 1, :], mv[:, 1, :, 1], EPS, None, ALU.add))
                own(pool.tensor_tensor(rstd[:, 1, :], var_eps[:, 1, :], half_pow[:, :], ALU.pow))

            def norm1(b):
                pool.wait_ge(s_st1, b + 1)
                wait(pool, s_job, job("T1", b - 1))
                if b >= 3:
                    wait(pool, s_jev, job("L2", b - 3))
                inv_std()
                for t in range(NT):
                    pool.tensor_scalar(x1_sb[:, t, :], x_sb[:, b % 2, t, :], mv[:, 0, t, 0:1],
                                       rstd[:, 0, t:t + 1], ALU.subtract, ALU.mult)
                own(pool.tensor_tensor(xb_sb[:, b % 3], x_sb[:, b % 2],
                                       bo_row[:, :].unsqueeze(1).broadcast_to([P, NT, D]), ALU.add))
                pool.sem_inc(s_x1, 1)

            def norm2(b):
                pool.wait_ge(s_st2, b + 1)
                wait(pool, s_job, job("TZ", b - 1))
                inv_std2()
                for t in range(NT):
                    last = pool.tensor_scalar(z_sb[:, t, :], x1_sb[:, t, :], mv[:, 1, t, 0:1],
                                              rstd[:, 1, t:t + 1], ALU.subtract, ALU.mult)
                last.then_inc(s_z, 1)

            def split(i, rounds, ready):
                pool.wait_ge(s_jev, ready)
                wait(pool, s_pw[i], 96 * (rounds - 1))
                own(pool.tensor_copy(piece[i][0][:, :], full[i][:, :]))
                own(pool.tensor_tensor(rest[:, :], full[i][:, :], piece[i][0][:, :], ALU.subtract))
                own(pool.tensor_copy(piece[i][1][:, :], rest[:, :]))
                pool.tensor_tensor(piece[i][2][:, :], rest[:, :], piece[i][1][:, :],
                                   ALU.subtract).then_inc(s_split[i], 1)
                pool.wait_ge(s_split[i], rounds)

            pool.wait_ge(s_w, 16 * N_SMALL)
            norm1(0)
            norm2(0)
            split(0, 1, job("P", 0))
            for it in range(-1, B):
                if it + 1 < B:
                    split(1, it + 2, job("Q", it + 1))
                    split(2, it + 2, job("K", it + 1))
                    split(0, it + 3, job("Q", it + 1))
                if it == -1:
                    pool.tensor_scalar(w0[:, :], k0_u8[:, 0, :], 2.0, None, ALU.mult)
                    own(pool.tensor_scalar(rest[:, :], k0_u8[:, 1, :], 2.0, None, ALU.mult))
                    own(pool.tensor_tensor(w0[:, :], w0[:, :], rest[:, :], ALU.subtract))
                    pool.tensor_scalar(w1[:, :, :], k1_u8[:, :, :], 2.0, -1.0, ALU.mult, ALU.add)
                    own(pool.tensor_scalar(w2[:, :, :], k2_u8[:, :, :], 2.0, -1.0, ALU.mult, ALU.add))
                    pool.sem_inc(s_wf, 1)
                if it + 2 < B:
                    norm1(it + 2)
                    norm2(it + 2)

        @block.scalar
        def _(act):
            act.wait_ge(s_w, 16 * N_SMALL)
            act.wait_ge(s_ones, 10)

            def take_job(name, b, c):
                k = job(name, b, c)
                act.wait_ge(s_job, k)
                if name == "P":
                    last = act.copy(full[0][:, :], ps_job[:, :])
                elif name == "T1":
                    wait(act, s_jev, job("L0", b - 2, C1 - 1))
                    last = act.copy(x1_t[:, b % 2].rearrange("p t c -> p (t c)"), ps_job[:, :])
                elif name == "TZ":
                    last = act.activation(z_t[:, :].rearrange("d (p t) -> d t p", t=NT),
                                          ps_job[:, :].rearrange("d (t p) -> d t p", t=NT),
                                          ACT.Identity, bias=BB, scale=G)
                elif name == "Q":
                    wait(act, s_split[0], b + 1)
                    wait(act, s_split[1], b)
                    act.activation(full[1][:, :], ps_job[:, :], ACT.Identity, bias=col2[:, 1:2], scale=1.0)
                    last = act.activation(full[0][:, :], ps_job[:, :], ACT.Identity, bias=col2[:, 0:1], scale=1.0)
                elif name == "K":
                    wait(act, s_split[2], b)
                    last = act.activation(full[2][:, :], ps_job[:, :], ACT.Identity, bias=BK, scale=1.0)
                elif name == "L0":
                    last = act.activation(h1[:, c, :], ps_job[:, :], ACT.Relu, scale=col2[:, 2:3])
                else:
                    return
                last.then_inc(s_jev, 1)

            for n in STEPS:
                u = unit(n, 0)
                if u is not None:
                    act.wait_ge(s_pos, 2 * u + 1)
                    if u >= N_POS:
                        act.wait_ge(s_out_w[u % N_POS], 16 * (u // N_POS))
                    act.copy(pos_sb[:, u % N_POS, 0:2, 0:S], ps_pos[:, :, :]).then_inc(s_pa, 1)
                m, p = unit(n, CONTENT_LAG), unit(n, TURN_LAG)

                def exp(t):
                    act.wait_ge(s_ttr, NT * m + t + 1)
                    act.activation(sc_sb[:, m % N_SC, t, :], sc_sb[:, m % N_SC, t, :], ACT.Exp,
                                   bias=nmax[:, m % N_SC, t:t + 1], scale=-1.0).then_inc(s_exp, 1)

                if m is not None:
                    exp(0)
                if p is not None:
                    act.wait_ge(s_pt, 2 * p + 1)
                    wait(act, s_av, 2 * p - N_PT + 1)
                    act.copy(pt_sb[:, 2 * p % N_PT], ps_pt[:, :, :]).then_inc(s_ta, 1)
                if m is not None:
                    exp(1)
                for j in jobs(n):
                    take_job(*j)
                if m is not None:
                    exp(2)
                    exp(3)
                o = unit(n, TURN_LAG + 1)
                if o is not None and o % 4 == 3:
                    act.wait_ge(s_av, 2 * o + 2)
                    wait(act, s_hw, 16 * 2 * NT * (o // H))
                    act.copy(o_sb[:, o % H - 3:o % H + 1, :], ps_av[:, :, :]).then_inc(s_oev, 1)

        @block.vector
        def _(dve):
            done = [0]

            def own(ins):
                done[0] += 1
                ins.then_inc(s_chain, 1)
                dve.wait_ge(s_chain, done[0])

            dve.memset(ps_av[:, :, :], 0.0).then_inc(s_ones, 1)
            dve.wait_ge(s_w, 16 * N_SMALL)
            dve.tensor_tensor(col2[:, 0:1], BQ, UB, ALU.add).then_inc(s_ones, 1)
            dve.tensor_tensor(col2[:, 1:2], BQ, VB, ALU.add).then_inc(s_ones, 1)
            dve.tensor_scalar(col2[:, 2:4], cols[:, 6:8], 2.0, None, ALU.mult).then_inc(s_ones, 1)
            dve.memset(nmax[:, :, :], 0.0).then_inc(s_ones, 3)
            dve.wait_ge(s_ones, 10)

            def norm_stats(b, k):
                src = (x_sb[:, b % 2], x1_sb[:, :, :])[k]
                if k == 0:
                    dve.wait_ge(s_x[b % 2], 16 * (b // 2 + 1))
                    wait(dve, s_x1, b)
                else:
                    dve.wait_ge(s_x1, b + 1)
                    wait(dve, s_z, b)
                for t in range(NT):
                    last = dve.bn_stats(stats[:, k, t, :], src[:, t, :])
                own(last)
                for t in range(NT):
                    last = dve.bn_aggr(mv[:, k, t, :], stats[:, k, t, :])
                last.then_inc((s_st1, s_st2)[k], 1)

            def take_job(name, b, c):
                k = job(name, b, c)
                if name not in ("V", "L1", "L2", "WO"):
                    return
                dve.wait_ge(s_job, k)
                if name == "V":
                    wait(dve, s_av, 2 * H * (b - 1))
                    last = dve.tensor_tensor(
                        v_sb[:, b % 2, :, :, 0:DH],
                        ps_job[:, :].rearrange("p (j h d) -> p j h d", j=NT, d=DH),
                        bv_row[:, :].rearrange("p (h d) -> p h d", d=DH).unsqueeze(1)
                        .broadcast_to([P, NT, H, DH]), ALU.add)
                elif name == "L1":
                    last = dve.tensor_scalar(h2[:, c, :], ps_job[:, :], col2[:, 3:4], 0.0, ALU.mult, ALU.max)
                elif name == "L2":
                    last = dve.scalar_tensor_tensor(
                        out=y_sb[:, b % 2].rearrange("p t c -> p (t c)"), in0=ps_job[:, :], scalar=S2,
                        in1=xb_sb[:, b % 3].rearrange("p t c -> p (t c)"), op0=ALU.mult, op1=ALU.add)
                else:
                    wait(dve, s_out, 16 * b)
                    last = dve.tensor_tensor(out_sb[:, :, :].rearrange("p t c -> p (t c)"), ps_job[:, :],
                                             y_sb[:, b % 2].rearrange("p t c -> p (t c)"), ALU.add)
                last.then_inc(s_jev, 1)

            norm_stats(0, 0)
            norm_stats(0, 1)
            for n in STEPS:
                it, slot = n // 16, n % 16
                m, p, u = unit(n, CONTENT_LAG), unit(n, TURN_LAG), unit(n, 0)

                def score(t):
                    dve.wait_ge(s_con, NT * m + t + 1)
                    if t == 0:
                        dve.wait_ge(s_in[m % N_SC], 16 * (m // N_SC + 1))
                    dve.tensor_tensor_reduce(sc_sb[:, m % N_SC, t, :], ps_con[:, t % 2, :],
                                             sc_sb[:, m % N_SC, t, :], -SCALE, BIG, ALU.add, ALU.min,
                                             nmax[:, m % N_SC, t:t + 1]).then_inc(s_ttr, 1)

                if m is not None:
                    score(0)
                    score(1)
                if u is not None:
                    dve.wait_ge(s_pos, 2 * u + 2)
                    if u >= N_POS:
                        dve.wait_ge(s_out_w[u % N_POS], 16 * (u // N_POS))
                    dve.tensor_copy(pos_sb[:, u % N_POS, 2:4, 0:S], ps_pos[:, :, :]).then_inc(s_pd, 1)
                for j in jobs(n):
                    take_job(*j)
                if m is not None:
                    score(2)
                    score(3)
                if p is not None:
                    dve.wait_ge(s_pt, 2 * p + 2)
                    wait(dve, s_av, 2 * p + 1 - N_PT + 1)
                    dve.tensor_copy(pt_sb[:, (2 * p + 1) % N_PT], ps_pt[:, :, :]).then_inc(s_td, 1)
                if it + 2 < B and slot in (8, 10):
                    norm_stats(it + 2, (slot - 8) // 2)
                if it >= 1 and slot == 11:
                    dve.wait_ge(s_hr, 32 * it)
                    own(dve.reciprocal(l_t[:, :], l_t[:, :]))
                    dve.tensor_tensor(o_t[:, :], o_t[:, :], l_t[:, :], ALU.mult).then_inc(s_on, 1)

        @block.tensor
        def _(pe):
            pe.wait_ge(s_w, 16 * N_SMALL)
            pe.wait_ge(s_ones, 10)

            def do_job(name, b, c):
                k = job(name, b, c)
                wait(pe, s_jev, k - 1)
                if name == "P":
                    last = pe.matmul(ps_job[:, :], w_sb["p"][:, :], pe_sb[:, :], start=True, stop=True)
                elif name in ("T1", "TZ"):
                    src, s = ((x1_sb, s_x1), (z_sb, s_z))[name == "TZ"]
                    pe.wait_ge(s, b + 1)
                    for t in range(NT):
                        last = pe.transpose(ps_job[:, t * P:(t + 1) * P], src[:, t, :], id_sb[:, :])
                elif name == "Q":
                    last = pe.matmul(ps_job[:, :], w_sb["q"][:, :],
                                     z_t[:, :].rearrange("d (p t) -> d t p", t=NT), start=True, stop=True)
                elif name == "K":
                    last = pe.matmul(ps_job[:, :], w_sb["k"][:, :], z_t[:, :], start=True, stop=True)
                elif name == "V":
                    for j in range(NT):
                        last = pe.matmul(ps_job[:, j * P:(j + 1) * P], z_t[:, j * P:(j + 1) * P],
                                         w_sb["v"][:, :], start=True, stop=True)
                elif name == "L0":
                    if b == 0 and c == 0:
                        pe.wait_ge(s_wf, 1)
                    last = pe.matmul(ps_job[:, :], w0[:, c * P:(c + 1) * P],
                                     x1_t[:, b % 2].rearrange("p t c -> p (t c)"), start=True, stop=True)
                elif name == "L1":
                    for a in range(C1):
                        last = pe.matmul(ps_job[:, :], w1[:, a, c * P:(c + 1) * P], h1[:, a, :],
                                         start=(a == 0), stop=(a == C1 - 1))
                elif name == "L2":
                    for t in range(NT):
                        for a in range(C2):
                            last = pe.matmul(ps_job[:, t * P:(t + 1) * P], h2[:, a, t * P:(t + 1) * P],
                                             w2[:, a, :], start=(a == 0), stop=(a == C2 - 1))
                else:
                    pe.wait_ge(s_on, b + 1)
                    for t in range(NT):
                        last = pe.matmul(ps_job[:, t * P:(t + 1) * P], o_t[:, t * P:(t + 1) * P],
                                         w_sb["o"][:, :], start=True, stop=True)
                last.then_inc(s_job, 1)

            def at(u):
                h = u % H
                base = 64 * (h % 2)
                return slice(base, base + KR), h // 2

            def positions(u, g):
                b, (rows, q) = u // H, at(u)
                if g == 0:
                    half = q // HALF
                    pe.wait_ge(s_stk[3][half], 32)
                    pe.wait_ge(s_stk[1][half], 32 * (b + 1))
                    wait(pe, s_pd, u)
                else:
                    pe.wait_ge(s_pa, u + 1)
                for i in range(2):
                    t = 2 * g + i
                    last = pe.matmul(ps_pos[:, i, :], QV[rows, q, t * P:(t + 1) * P], PP[rows, q, :],
                                     start=True, stop=True)
                last.then_inc(s_pos, 1)

            def content(u, g):
                b, (rows, q) = u // H, at(u)
                if g == 0:
                    half = q // HALF
                    pe.wait_ge(s_stk[0][half], 32 * (b + 1))
                    pe.wait_ge(s_stk[2][half], 32 * (b + 1))
                for t in (2 * g, 2 * g + 1):
                    wait(pe, s_ttr, NT * u + t - 1)
                    pe.matmul(ps_con[:, t % 2, :], QU[rows, q, t * P:(t + 1) * P], KK[rows, q, :],
                              start=True, stop=True).then_inc(s_con, 1)

            def turn(u, g):
                if g == 0:
                    pe.wait_ge(s_exp, NT * (u + 1))
                    wait(pe, s_td, u)
                else:
                    pe.wait_ge(s_ta, u + 1)
                for i in range(2):
                    j = 2 * g + i
                    for t in range(NT):
                        last = pe.transpose(ps_pt[:, i, t * P:(t + 1) * P],
                                            sc_sb[:, u % N_SC, t, j * P:(j + 1) * P], id_sb[:, :])
                last.then_inc(s_pt, 1)

            def values(u, g):
                b, h = u // H, u % H
                pe.wait_ge((s_ta, s_td)[g], u + 1)
                if g == 0:
                    if h == 0:
                        pe.wait_ge(s_jev, job("V", b))
                    if h % 4 == 0:
                        wait(pe, s_oev, u // 4)
                for i in range(2):
                    j = 2 * g + i
                    for t in range(NT):
                        last = pe.matmul(ps_av[32 * t:32 * t + 2 * DH, h % 4, :], v_sb[:, b % 2, j, h, :],
                                         pt_sb[:, (2 * u + g) % N_PT, i, t * P:(t + 1) * P],
                                         start=(j == 0), stop=(j == NT - 1))
                last.then_inc(s_av, 1)

            for n in STEPS:
                u, m, p, o = unit(n, 0), unit(n, CONTENT_LAG), unit(n, TURN_LAG), unit(n, TURN_LAG + 1)
                if u is not None:
                    positions(u, 0)
                if m is not None:
                    content(m, 0)
                if p is not None:
                    turn(p, 0)
                if o is not None:
                    values(o, 1)
                for j in jobs(n):
                    do_job(*j)
                if u is not None:
                    positions(u, 1)
                if m is not None:
                    content(m, 1)
                if p is not None:
                    turn(p, 1)
                    values(p, 0)


N_SMALL = 21
BIG = 3.4e38


def kernel(**inputs):
    import numpy as np
    import concourse.bacc as bacc
    from concourse.bass_utils import run_bass_kernel_spmd

    D, S, H, DH = 128, 512, 16, 8

    def perm(a):
        a = np.asarray(a)
        lead = a.shape[:-1]
        return np.ascontiguousarray(
            np.moveaxis(a.reshape(*lead, H // 2, 2, DH), -3, -1).reshape(*lead, D))

    pos = np.arange(S, dtype=np.float32)[:, None]
    div = np.exp(np.arange(0, D, 2, dtype=np.float32) * np.float32(-np.log(10000.0) / D)).astype(np.float32)
    ang = (pos * div).astype(np.float32)
    pe = np.stack([np.sin(ang), np.cos(ang)], axis=-1).reshape(S, D).astype(np.float32)

    g = {k[3:]: np.asarray(v) for k, v in inputs.items()}
    data = {
        "x": g["attn_x"], "ln_g": g["attn_ln_g"], "ln_b": g["attn_ln_b"],
        "wq": perm(g["attn_Wq"]), "bq": perm(g["attn_bq"]), "wk": perm(g["attn_Wk"]), "bk": perm(g["attn_bk"]),
        "wv": g["attn_Wv"], "bv": g["attn_bv"], "wp": perm(g["attn_Wp"]), "wo": g["attn_Wo"], "bo": g["attn_bo"],
        "u_bias": perm(g["attn_u_bias"].reshape(D)), "v_bias": perm(g["attn_v_bias"].reshape(D)),
        "k0": g["ffn_k0"], "k1": g["ffn_k1"], "k2": g["ffn_k2"],
        "s0": g["ffn_s0"].reshape(1), "s1": g["ffn_s1"].reshape(1), "s2": g["ffn_s2"].reshape(1),
        "pe_t": np.ascontiguousarray(pe.T), "ident": np.eye(D, dtype=np.float32),
    }
    nc = bacc.Bacc("TRN2", target_bir_lowering=False, num_devices=1)
    arrays, args = {}, []
    for name, a in data.items():
        a = np.ascontiguousarray(a)
        arrays[f"in_{name}"] = a
        args.append(nc.dram_tensor(f"in_{name}", a.shape, mybir.dt.from_np(a.dtype), kind="ExternalInput").ap())
    out = nc.dram_tensor("out", g["attn_x"].shape, F32, kind="ExternalOutput").ap()
    attention_mlp(nc, *args, out)
    r = run_bass_kernel_spmd(nc, [arrays], core_ids=[0])
    return r.results[0]["out"]
```

```python
from contextlib import ExitStack

import concourse.bass as bass
from concourse import mybir

ALU = mybir.AluOpType
ACT = mybir.ActivationFunctionType
F32 = mybir.dt.float32
BF16 = mybir.dt.bfloat16
F32R = mybir.dt.float32r
U8 = mybir.dt.uint8

P = 128
EPS = 1e-5
Q_PIECES = (0, 0, 0, 1, 1, 2)
K_PIECES = (2, 0, 1, 0, 1, 0)
NR = len(Q_PIECES)


def attention_mlp(nc, x, ln_g, ln_b, wq, bq, wk, bk, wv, bv, wp, wo, bo, u_bias, v_bias,
                  k0, k1, k2, s0, s1, s2, pe_t, ident, out):
    B, S, D = x.shape
    H, DH = 16, 8
    assert D == P and H * DH == P and S == 512 and k0.shape[1] == S
    NT = S // P
    UNITS = B * H
    PAIRS = H // 2
    KR = NR * DH
    HALF = PAIRS // 2
    F1, F2 = k0.shape[1], k1.shape[1]
    C1, C2 = F1 // P, F2 // P
    SCALE = float(DH) ** -0.5
    PITCH = S + 1

    SHIFT_LAG = 2
    CONTENT_LAG = 4
    TURN_LAG = CONTENT_LAG + 1
    N_POS = 2
    N_SC = 4
    N_SHIFT = 4
    N_PT = 4
    VALUES_LAG = 2

    shift = nc.dram_tensor("shift", [N_SHIFT, S * PITCH], F32, kind="Internal").ap()
    stk = [nc.dram_tensor(f"stk_{n}", [2, NR, DH * PAIRS, S], BF16, kind="Internal").ap()
           for n in ("qu", "qv", "k", "p")]
    heads_d = nc.dram_tensor("heads_d", [P, NT, P], F32, kind="Internal").ap()
    sums_d = nc.dram_tensor("sums_d", [P, NT, P], F32, kind="Internal").ap()

    with ExitStack() as ctx:
        def sb(name, shape, dt=F32):
            return ctx.enter_context(nc.sbuf_tensor(name, shape, dt))

        def psum(name, shape):
            return ctx.enter_context(nc.psum_tensor(name, shape, F32))

        def sem(name):
            return ctx.enter_context(nc.semaphore(name))

        id_sb = sb("id_sb", [P, P])
        w_sb = {n: sb(f"w_{n}", [P, D]) for n in ("q", "k", "v", "o")}
        cols = sb("cols", [P, 10])
        G, BB, BQ, BK, UB, VB, BO, S0, S1, S2 = (cols[:, i:i + 1] for i in range(10))
        col2 = sb("col2", [P, 4])
        bv_row = sb("bv_row", [P, D])
        w0 = sb("w0", [P, F1], F32R)
        w1 = sb("w1", [P, C1, F2], F32R)
        w2 = sb("w2", [P, C2, D], F32R)
        half_pow = sb("half_pow", [P, NT])

        x_sb = sb("x_sb", [P, 2, NT, D])
        xr_sb = sb("xr_sb", [P, NT, D])
        x1_sb = sb("x1_sb", [P, NT, D])
        z_sb = sb("z_sb", [P, NT, D])
        stats = sb("stats", [P, 2, NT, 6])
        mv = sb("mv", [P, 2, NT, 2])
        var_eps = sb("var_eps", [P, 2, NT])
        rstd = sb("rstd", [P, 2, NT])
        x1_t = sb("x1_t", [P, 2, 2, S], F32R)
        z_t = sb("z_t", [P, S])
        full = [sb(f"full_{n}", [P, S]) for n in ("qu", "qv", "k")]
        pe_sb = full[1]
        rest = sb("rest", [P, S])
        piece = [sb(f"piece{i}", [P, 3, S], BF16) for i in range(3)]
        stack = [sb(f"stack_{n}", [P, PAIRS, S], BF16) for n in ("qu", "qv", "k", "p")]
        QU, QV, KK, PP = stack
        v_sb = sb("v_sb", [P, 2, NT, H, 2 * DH])

        pos_sb = sb("pos_sb", [P, N_POS, NT, PITCH])
        sc_sb = sb("sc_sb", [P, N_SC, NT, S])
        nmax = sb("nmax", [P, N_SC, NT])
        pt_sb = sb("pt_sb", [P, N_PT, S])
        o_sb = sb("o_sb", [P, H, P])
        o_t = sb("o_t", [P, S])
        l_t = sb("l_t", [P, S])

        stage = pt_sb[:, :, :].rearrange("p a c -> p (a c)").bitcast(U8)
        k0_u8 = stage[:, 0:2 * F1].rearrange("p (a n) -> p a n", a=2)
        k1_u8 = stage[:, 2 * F1:2 * F1 + C1 * F2].rearrange("p (a n) -> p a n", a=C1)
        k2_u8 = stage[:, 2 * F1 + C1 * F2:2 * F1 + C1 * F2 + C2 * D].rearrange("p (a n) -> p a n", a=C2)
        act_sb = sb("act_sb", [P, 2, S])
        w_sb["p"] = act_sb[:, 0, 0:D]
        h1 = sb("h1", [P, C1, 2, S], F32R)
        h2 = sb("h2", [P, C2, 2, S], F32R)
        y_t = sb("y_t", [P, S])

        ps_pos = psum("ps_pos", [P, 2, S])
        ps_con = psum("ps_con", [P, 2, S])
        ps_pt = psum("ps_pt", [P, 2, S])
        ps_av = psum("ps_av", [P, 4, P])
        ps_job = psum("ps_job", [P, S])

        s_w = sem("s_w")
        s_ones = sem("s_ones")
        s_wf = sem("s_wf")
        s_x = [sem("s_x0"), sem("s_x1")]
        s_chain = sem("s_chain")
        s_pool = sem("s_pool")
        s_st1, s_st2 = sem("s_st1"), sem("s_st2")
        s_x1, s_z = sem("s_x1n"), sem("s_z")
        s_job = sem("s_job")
        s_jev = sem("s_jev")
        s_split = sem("s_split")
        s_pw = [sem(f"s_pw{i}") for i in range(3)]
        s_stk = [[sem(f"s_stk{i}{j}") for j in range(2)] for i in range(4)]
        s_pos, s_con, s_pt, s_av = sem("s_pos"), sem("s_con"), sem("s_pt"), sem("s_av")
        s_pe = sem("s_pe")
        s_out_w = [sem(f"s_pout{i}") for i in range(N_POS)]
        s_in = [sem(f"s_in{i}") for i in range(N_SC)]
        s_ttr, s_exp = sem("s_ttr"), sem("s_exp")
        s_te = sem("s_te")
        s_oev = sem("s_oev")
        s_hw, s_hr = sem("s_hw"), sem("s_hr")
        s_inv = sem("s_inv")
        s_on = sem("s_on")
        s_out = sem("s_out")
        s_xr = sem("s_xr")
        s_act = sem("s_act")
        s_hl = sem("s_hl")

        def wait(eng, s, n):
            if n > 0:
                eng.wait_ge(s, n)

        SLOT = {}
        order = []

        def add(step, name, b, c=0):
            SLOT.setdefault(step, []).append((name, b, c))

        NEXT = ((0, "T1"), (2, "TZ"), (4, "Q"), (6, "K"), (9, "V"))
        for it in range(-1, B + 1):
            at = 16 * it
            if it == -1:
                add(at, "P", 0)
            if it + 1 < B:
                for slot, n in NEXT:
                    add(at + slot, n, it + 1)
            if 0 <= it < B:
                for c in range(C1):
                    add(at + 1 + 2 * c, "L0", it, c)
                for c in range(C2):
                    add(at + 8 + 2 * c, "L1", it, c)
                add(at + 15, "L2", it)
            if it >= 1:
                add(at + 11, "WO", it - 1)
                add(at + 13, "TY", it - 1)
        STEPS = range(-16, 16 * B + 16)
        for n in STEPS:
            order += SLOT.get(n, [])
        JOB = {j: i + 1 for i, j in enumerate(order)}

        def jobs(n):
            return SLOT.get(n, [])

        def job(name, b, c=0):
            return JOB[(name, b, c)] if b >= 0 else 0

        SPLIT = {(3, 0): 0}
        for b in range(B):
            for i in (1, 0, 2):
                SPLIT[(i, b)] = len(SPLIT)
        PIECES_OUT = {(3, 0): 96}
        for b in range(-1, B):
            for i in range(3):
                PIECES_OUT[(i, b)] = 96 * (b + 1 + (i == 0))
        ACTS = {}
        for j in order:
            if j[0] in ("T1", "L0", "L1"):
                ACTS[j] = len(ACTS)

        def two(name, b, c):
            return {"T1": x1_t[:, b % 2], "L0": h1[:, c], "L1": h2[:, c]}[name]

        def wait_two(eng, name, b, c):
            wait(eng, s_hl, ACTS[(name, b, c)] - 1)
            wait(eng, s_job, {"T1": job("L0", b - 2, C1 - 1), "L0": job("L1", b - 1, C2 - 1),
                              "L1": job("L2", b - 1)}[name])

        def unit(n, lag):
            return n - lag if 0 <= n - lag < UNITS else None

        block = ctx.enter_context(nc.Block())

        @block.sync
        def _(sp):
            def load_x(b):
                wait(sp, s_x1, b - 1)
                sp.dma_start(x_sb[:, b % 2], x[b].rearrange("(p t) d -> p t d", t=NT)) \
                  .then_inc(s_x[b % 2], 16)

            def row(v, n):
                return bass.AP(tensor=v.tensor, offset=0, ap=[[0, P], [1, n]])

            load_x(0)
            small = [(id_sb[:, :], ident), (w_sb["p"][:, :], wp), (pe_sb[:, :], pe_t),
                     (w_sb["q"][:, :], wq), (w_sb["k"][:, :], wk), (w_sb["v"][:, :], wv),
                     (w_sb["o"][:, :], wo)]
            small += [(cols[:, i:i + 1], v.rearrange("(p a) -> p a", a=1))
                      for i, v in enumerate((ln_g, ln_b, bq, bk, u_bias, v_bias, bo))]
            small += [(cols[:, 7 + i:8 + i], row(v, 1)) for i, v in enumerate((s0, s1, s2))]
            small += [(bv_row[:, :], row(bv, D)),
                      (k0_u8[:, :, :], k0.rearrange("(a p) n -> p a n", p=P)),
                      (k1_u8[:, :, :], k1.rearrange("(a p) n -> p a n", p=P)),
                      (k2_u8[:, :, :], k2.rearrange("(a p) n -> p a n", p=P))]
            assert len(small) == N_SMALL
            for dst, src in small:
                sp.dma_start(dst, src).then_inc(s_w, 16)
            load_x(1)

            def write_pieces(i, b, which, dst):
                k = SPLIT[(i, b)]
                wait(sp, s_split, k + 1)
                for n in range(3):
                    at = [r for r in range(NR) if which[r] == n]
                    step = at[1] - at[0] if len(at) > 1 else 1
                    for par in range(2):
                        d = dst[par, at[0]:at[-1] + 1:step].rearrange("r q c -> q r c")
                        s = piece[i % 3][64 * par:64 * par + 64, n, :].unsqueeze(1) \
                            .broadcast_to([64, len(at), S])
                        sp.dma_start(d, s).then_inc(s_pw[i % 3], 16)

            def read_stack(j, b, half):
                sp.wait_ge(s_pw[j % 3], PIECES_OUT[(j, b)])
                for par in range(2):
                    src = stk[j][par].rearrange("r (d q) c -> (r d) q c", q=PAIRS)
                    q = slice(HALF * half, HALF * half + HALF)
                    sp.dma_start(stack[j][64 * par:64 * par + KR, q, :], src[:, q, :]) \
                      .then_inc(s_stk[j][half], 16)

            for n in STEPS:
                it, slot = n // 16, n % 16
                if it == -1 and slot == 1:
                    write_pieces(3, 0, K_PIECES, stk[3])
                    read_stack(3, 0, 0)
                    read_stack(3, 0, 1)
                if it >= 1 and slot == 8:
                    wait(sp, s_out, 16 * (it - 1))
                    sp.dma_start(xr_sb[:, :, :], x[it - 1].rearrange("(p t) d -> p t d", t=NT)) \
                      .then_inc(s_xr, 16)
                if it >= 2 and slot == 1:
                    wait(sp, s_jev, job("TY", it - 2))
                    sp.dma_start(out[it - 2].rearrange("(p t) d -> p t d", t=NT),
                                 xr_sb[:, :, :]).then_inc(s_out, 16)
                if 0 <= it < B and slot == CONTENT_LAG:
                    wait(sp, s_con, 4 * 16 * it)
                    for i in range(3):
                        read_stack(i, it, 1)
                for i, w, at in ((1, Q_PIECES, 6), (0, Q_PIECES, 7), (2, K_PIECES, 8)):
                    if it + 1 < B and slot == at:
                        if it >= 0:
                            for half in range(2):
                                sp.wait_ge(s_stk[i][half], 32 * (it + 1))
                        write_pieces(i, it + 1, w, stk[i])
                if it + 1 < B and slot == CONTENT_LAG + 8:
                    wait(sp, s_con, 4 * (16 * it + 8))
                    for i in range(3):
                        read_stack(i, it + 1, 0)
                if it >= 1 and slot == TURN_LAG + 2:
                    sp.wait_ge(s_oev, 4 * it)
                    for part, dst in enumerate((heads_d, sums_d)):
                        for t in range(NT):
                            rows = slice(32 * t + DH * part, 32 * t + DH * part + DH)
                            sp.dma_start(dst[:, t, :].rearrange("(h d) c -> d h c", d=DH), o_sb[rows, :, :]) \
                              .then_inc(s_hw, 16)
                if it >= 1 and slot == TURN_LAG + 3:
                    sp.wait_ge(s_hw, 16 * 2 * NT * it)
                    wait(sp, s_job, job("WO", it - 2))
                    sp.dma_start(o_t[:, :], heads_d.rearrange("p t c -> p (t c)")).then_inc(s_hr, 16)
                    sp.dma_start(l_t[:, :], sums_d.rearrange("p t c -> p (t c)")).then_inc(s_hr, 16)
                if it + 3 < B and slot == 13:
                    load_x(it + 3)
                u = unit(n, SHIFT_LAG)
                if u is not None:
                    sp.wait_ge(s_out_w[u % N_POS], 16 * (u // N_POS + 1))
                    wait(sp, s_pt, NT * (u - N_SC + 1))
                    sp.dma_start(sc_sb[:, u % N_SC].rearrange("p t c -> p (t c)"),
                                 shift[u % N_SHIFT, S - 1:S - 1 + S * S].rearrange("(p c) -> p c", p=P)) \
                      .then_inc(s_in[u % N_SC], 16)
                u = unit(n, 0)
                if u is not None:
                    sp.wait_ge(s_pe, NT * (u + 1))
                    if u >= N_SHIFT:
                        v = u - N_SHIFT
                        sp.wait_ge(s_in[v % N_SC], 16 * (v // N_SC + 1))
                    sp.dma_start(shift[u % N_SHIFT].rearrange("(p c) -> p c", p=P),
                                 pos_sb[:, u % N_POS].rearrange("p t c -> p (t c)")) \
                      .then_inc(s_out_w[u % N_POS], 16)
            wait(sp, s_jev, job("TY", B - 1))
            if B >= 1:
                sp.dma_start(out[B - 1].rearrange("(p t) d -> p t d", t=NT), xr_sb[:, :, :]) \
                  .then_inc(s_out, 16)
            sp.wait_ge(s_out, 16 * B)

        @block.gpsimd
        def _(pool):
            done = [0]

            def own(ins):
                done[0] += 1
                ins.then_inc(s_pool, 1)
                pool.wait_ge(s_pool, done[0])

            pool.memset(half_pow[:, :], -0.5).then_inc(s_ones, 1)
            pool.memset(pos_sb[:, :, :, S:PITCH], 0.0).then_inc(s_ones, 1)
            pool.memset(v_sb[:, :, :, :, DH:2 * DH], 1.0).then_inc(s_ones, 1)
            pool.wait_ge(s_ones, 3)

            def inv_std():
                own(pool.tensor_scalar(var_eps[:, 0, :], mv[:, 0, :, 1], EPS, None, ALU.add))
                own(pool.tensor_tensor(rstd[:, 0, :], var_eps[:, 0, :], half_pow[:, :], ALU.pow))

            def inv_std2():
                own(pool.tensor_scalar(var_eps[:, 1, :], mv[:, 1, :, 1], EPS, None, ALU.add))
                own(pool.tensor_tensor(rstd[:, 1, :], var_eps[:, 1, :], half_pow[:, :], ALU.pow))

            def norm1(b):
                pool.wait_ge(s_st1, b + 1)
                wait(pool, s_job, job("T1", b - 1))
                inv_std()
                for t in range(NT):
                    last = pool.tensor_scalar(x1_sb[:, t, :], x_sb[:, b % 2, t, :], mv[:, 0, t, 0:1],
                                              rstd[:, 0, t:t + 1], ALU.subtract, ALU.mult)
                last.then_inc(s_x1, 1)

            def norm2(b):
                pool.wait_ge(s_st2, b + 1)
                wait(pool, s_job, job("TZ", b - 1))
                inv_std2()
                for t in range(NT):
                    last = pool.tensor_scalar(z_sb[:, t, :], x1_sb[:, t, :], mv[:, 1, t, 0:1],
                                              rstd[:, 1, t:t + 1], ALU.subtract, ALU.mult)
                last.then_inc(s_z, 1)

            def split(i, b, ready):
                k = SPLIT[(i, b)]
                src, pc = full[i % 3], piece[i % 3]
                pool.wait_ge(s_jev, ready)
                pool.tensor_tensor(rest[:, :], src[:, :], pc[:, 0, :], ALU.subtract)
                own(pool.tensor_tensor(pc[:, 1, :], src[:, :], pc[:, 0, :], ALU.subtract))
                pool.tensor_tensor(pc[:, 2, :], rest[:, :], pc[:, 1, :], ALU.subtract).then_inc(s_split, 1)
                pool.wait_ge(s_split, k + 1)

            def split2(name, b, c):
                k, dst = ACTS[(name, b, c)], two(name, b, c)
                pool.wait_ge(s_jev, job(name, b, c))
                pool.tensor_tensor(dst[:, 1, :], act_sb[:, k % 2, :], dst[:, 0, :].bitcast(F32), ALU.subtract) \
                    .then_inc(s_hl, 1)

            pool.wait_ge(s_w, 16 * N_SMALL)
            norm1(0)
            norm2(0)
            split(3, 0, job("P", 0))
            for n in STEPS:
                it, slot = n // 16, n % 16
                for name, b, c in jobs(n):
                    if name in ("T1", "L0", "L1"):
                        split2(name, b, c)
                    elif name == "Q":
                        split(1, b, job("Q", b))
                        split(0, b, job("Q", b))
                    elif name == "K":
                        split(2, b, job("K", b))
                if it == -1 and slot == 7:
                    pool.tensor_scalar(w0[:, :], k0_u8[:, 0, :], 2.0, None, ALU.mult)
                    own(pool.tensor_scalar(rest[:, :], k0_u8[:, 1, :], 2.0, None, ALU.mult))
                    pool.tensor_tensor(w0[:, :], w0[:, :].bitcast(F32), rest[:, :], ALU.subtract)
                    pool.tensor_scalar(w1[:, :, :], k1_u8, 2.0, -1.0, ALU.mult, ALU.add)
                    own(pool.tensor_scalar(w2[:, :, :], k2_u8, 2.0, -1.0, ALU.mult, ALU.add))
                    pool.sem_inc(s_wf, 1)
                if it >= 1 and slot == 9:
                    pool.wait_ge(s_inv, NT * it)
                    pool.tensor_tensor(o_t[:, :], o_t[:, :], l_t[:, :], ALU.mult).then_inc(s_on, 1)
                if it + 2 < B and slot == 9:
                    norm1(it + 2)
                if it + 2 < B and slot == 11:
                    norm2(it + 2)

        @block.scalar
        def _(act):
            act.wait_ge(s_w, 16 * N_SMALL)
            act.wait_ge(s_ones, 10)

            def take_job(name, b, c):
                k = job(name, b, c)
                act.wait_ge(s_job, k)
                if name == "P":
                    act.copy(piece[0][:, 0, :], ps_job[:, :])
                    last = act.copy(full[0][:, :], ps_job[:, :])
                elif name == "T1":
                    wait_two(act, name, b, c)
                    act.copy(x1_t[:, b % 2, 0, :], ps_job[:, :])
                    last = act.copy(act_sb[:, ACTS[(name, b, c)] % 2, :], ps_job[:, :])
                elif name == "TZ":
                    last = act.activation(z_t[:, :].rearrange("d (p t) -> d t p", t=NT),
                                          ps_job[:, :].rearrange("d (t p) -> d t p", t=NT),
                                          ACT.Identity, bias=BB, scale=G)
                elif name in ("Q", "K"):
                    for i in {"Q": (1, 0), "K": (2,)}[name]:
                        bias = (col2[:, 0:1], col2[:, 1:2], BK)[i]
                        wait(act, s_split, SPLIT[(i, b - 1)] + 1 if b else 1)
                        wait(act, s_pw[i], PIECES_OUT[(i, b - 1)])
                        act.activation(piece[i][:, 0, :], ps_job[:, :], ACT.Identity, bias=bias, scale=1.0)
                        last = act.activation(full[i][:, :], ps_job[:, :], ACT.Identity, bias=bias, scale=1.0)
                elif name in ("L0", "L1"):
                    wait_two(act, name, b, c)
                    k = ("L0", "L1").index(name)
                    for dst in (two(name, b, c)[:, 0, :], act_sb[:, ACTS[(name, b, c)] % 2, :]):
                        last = act.activation(dst, ps_job[:, :], ACT.Relu, scale=col2[:, 2 + k:3 + k])
                elif name == "L2":
                    wait(act, s_job, job("TY", b - 1))
                    last = act.activation(y_t[:, :], ps_job[:, :], ACT.Identity, bias=BO, scale=S2)
                else:
                    return
                last.then_inc(s_jev, 1)

            for n in STEPS:
                u, m = unit(n, 0), unit(n, CONTENT_LAG)
                for t in range(NT):
                    if u is not None:
                        act.wait_ge(s_pos, NT * u + t + 1)
                        if t == 0 and u >= N_POS:
                            act.wait_ge(s_out_w[u % N_POS], 16 * (u // N_POS))
                        act.copy(pos_sb[:, u % N_POS, t, 0:S], ps_pos[:, t % 2, :]).then_inc(s_pe, 1)
                    if m is not None:
                        act.wait_ge(s_ttr, NT * m + t + 1)
                        act.activation(sc_sb[:, m % N_SC, t, :], sc_sb[:, m % N_SC, t, :], ACT.Exp,
                                       bias=nmax[:, m % N_SC, t:t + 1], scale=-1.0).then_inc(s_exp, 1)
                    q = NT * (n - TURN_LAG) + t - VALUES_LAG
                    o = q // NT
                    if 0 <= o < UNITS and q % NT == NT - 1 and o % 4 == 3:
                        act.wait_ge(s_av, NT * (o + 1))
                        wait(act, s_hw, 16 * 2 * NT * (o // H))
                        act.copy(o_sb[:, o % H - 3:o % H + 1, :], ps_av[:, :, :]).then_inc(s_oev, 1)
                for j in jobs(n):
                    take_job(*j)

        @block.vector
        def _(dve):
            done = [0]

            def own(ins):
                done[0] += 1
                ins.then_inc(s_chain, 1)
                dve.wait_ge(s_chain, done[0])

            dve.memset(ps_av[:, :, :], 0.0).then_inc(s_ones, 1)
            dve.wait_ge(s_w, 16 * N_SMALL)
            dve.tensor_tensor(col2[:, 0:1], BQ, UB, ALU.add).then_inc(s_ones, 1)
            dve.tensor_tensor(col2[:, 1:2], BQ, VB, ALU.add).then_inc(s_ones, 1)
            dve.tensor_scalar(col2[:, 2:4], cols[:, 7:9], 2.0, None, ALU.mult).then_inc(s_ones, 1)
            dve.memset(nmax[:, :, :], 0.0).then_inc(s_ones, 3)
            dve.wait_ge(s_ones, 10)

            def norm_stats(b, k):
                src = (x_sb[:, b % 2], x1_sb[:, :, :])[k]
                if k == 0:
                    dve.wait_ge(s_x[b % 2], 16 * (b // 2 + 1))
                    wait(dve, s_x1, b)
                else:
                    dve.wait_ge(s_x1, b + 1)
                    wait(dve, s_z, b)
                for t in range(NT):
                    last = dve.bn_stats(stats[:, k, t, :], src[:, t, :])
                own(last)
                for t in range(NT):
                    last = dve.bn_aggr(mv[:, k, t, :], stats[:, k, t, :])
                last.then_inc((s_st1, s_st2)[k], 1)

            def take_job(name, b, c):
                k = job(name, b, c)
                if name not in ("V", "WO", "TY"):
                    return
                dve.wait_ge(s_job, k)
                if name == "V":
                    wait(dve, s_av, NT * H * (b - 1))
                    last = dve.tensor_tensor(
                        v_sb[:, b % 2, :, :, 0:DH],
                        ps_job[:, :].rearrange("p (j h d) -> p j h d", j=NT, d=DH),
                        bv_row[:, :].rearrange("p (h d) -> p h d", d=DH).unsqueeze(1)
                        .broadcast_to([P, NT, H, DH]), ALU.add)
                elif name == "WO":
                    last = dve.tensor_tensor(y_t[:, :], ps_job[:, :], y_t[:, :], ALU.add)
                else:
                    dve.wait_ge(s_xr, 16 * (b + 1))
                    last = dve.tensor_tensor(xr_sb[:, :, :].rearrange("p t c -> p (t c)"), ps_job[:, :],
                                             xr_sb[:, :, :].rearrange("p t c -> p (t c)"), ALU.add)
                last.then_inc(s_jev, 1)

            norm_stats(0, 0)
            norm_stats(0, 1)
            for n in STEPS:
                it, slot = n // 16, n % 16
                m, p = unit(n, CONTENT_LAG), unit(n, TURN_LAG)
                for t in range(NT):
                    if m is not None:
                        dve.wait_ge(s_con, NT * m + t + 1)
                        if t == 0:
                            dve.wait_ge(s_in[m % N_SC], 16 * (m // N_SC + 1))
                        dve.tensor_tensor_reduce(sc_sb[:, m % N_SC, t, :], ps_con[:, t % 2, :],
                                                 sc_sb[:, m % N_SC, t, :], -SCALE, BIG, ALU.add, ALU.min,
                                                 nmax[:, m % N_SC, t:t + 1]).then_inc(s_ttr, 1)
                    if p is not None:
                        q = NT * p + t
                        dve.wait_ge(s_pt, q + 1)
                        if q == 0:
                            dve.wait_ge(s_wf, 1)
                        wait(dve, s_av, q - N_PT + 1)
                        dve.tensor_copy(pt_sb[:, q % N_PT], ps_pt[:, t % 2, :]).then_inc(s_te, 1)
                    if it >= 1 and slot == 9:
                        if t == 0:
                            dve.wait_ge(s_hr, 32 * it)
                        cut = slice(t * P, (t + 1) * P)
                        dve.reciprocal(l_t[:, cut], l_t[:, cut]).then_inc(s_inv, 1)
                for j in jobs(n):
                    take_job(*j)
                if it + 2 < B and slot in (8, 10):
                    norm_stats(it + 2, (slot - 8) // 2)

        @block.tensor
        def _(pe):
            pe.wait_ge(s_w, 16 * N_SMALL)
            pe.wait_ge(s_ones, 10)

            def job_parts(name, b, c):
                if name == "P":
                    return [lambda: pe.matmul(ps_job[:, :], w_sb["p"][:, :], pe_sb[:, :], start=True, stop=True)]
                if name == "Q":
                    return [lambda: pe.matmul(ps_job[:, :], w_sb["q"][:, :],
                                              z_t[:, :].rearrange("d (p t) -> d t p", t=NT), start=True, stop=True)]
                if name == "K":
                    return [lambda: pe.matmul(ps_job[:, :], w_sb["k"][:, :], z_t[:, :], start=True, stop=True)]
                if name == "WO":
                    def heads_out():
                        pe.wait_ge(s_on, b + 1)
                        return pe.matmul(ps_job[:, :], w_sb["o"][:, :], o_t[:, :], start=True, stop=True)
                    return [heads_out]
                if name in ("T1", "TZ", "V", "TY"):
                    def block(t):
                        dst, cut = ps_job[:, t * P:(t + 1) * P], slice(t * P, (t + 1) * P)
                        if name == "V":
                            return pe.matmul(dst, z_t[:, cut], w_sb["v"][:, :], start=True, stop=True)
                        if name == "TY":
                            return pe.transpose(dst, y_t[:, cut], id_sb[:, :])
                        src, ready = ((x1_sb, s_x1), (z_sb, s_z))[name == "TZ"]
                        if t == 0:
                            pe.wait_ge(ready, b + 1)
                        return pe.transpose(dst, src[:, t, :], id_sb[:, :])
                    return [lambda t=t: block(t) for t in range(NT)]
                w, src, before = {"L0": (w0, x1_t[:, b % 2].unsqueeze(1), [("T1", b, 0)]),
                                  "L1": (w1, h1, [("L0", b, a) for a in range(C1)]),
                                  "L2": (w2, h2, [("L1", b, a) for a in range(C2)])}[name]

                def product(a, hl):
                    if name == "L0" and b == 0 and c == 0:
                        pe.wait_ge(s_wf, 1)
                    if hl == 0:
                        pe.wait_ge(s_hl, ACTS[before[a]] + 1)
                    lhs = w[:, c * P:(c + 1) * P] if name == "L0" else w[:, a, c * P:(c + 1) * P]
                    return pe.matmul(ps_job[:, :], lhs, src[:, a, hl, :],
                                     start=(a == 0 and hl == 0), stop=(a == len(before) - 1 and hl == 1))
                return [lambda a=a, hl=hl: product(a, hl) for a in range(len(before)) for hl in range(2)]

            def do_job(name, b, c, part):
                k, todo = job(name, b, c), job_parts(name, b, c)
                first, end = (-(-len(todo) * i // JOB_PARTS) for i in (part, part + 1))
                if part == 0:
                    wait(pe, s_jev, k - 1)
                for i in range(first, end):
                    last = todo[i]()
                if first < end == len(todo):
                    last.then_inc(s_job, 1)

            def at(u):
                h = u % H
                base = 64 * (h % 2)
                return slice(base, base + KR), h // 2

            def positions(u, t):
                b, (rows, q) = u // H, at(u)
                if t == 0:
                    half = q // HALF
                    pe.wait_ge(s_stk[3][half], 32)
                    pe.wait_ge(s_stk[1][half], 32 * (b + 1))
                wait(pe, s_pe, NT * u + t - 1)
                pe.matmul(ps_pos[:, t % 2, :], QV[rows, q, t * P:(t + 1) * P], PP[rows, q, :],
                          start=True, stop=True).then_inc(s_pos, 1)

            def content(u, t):
                b, (rows, q) = u // H, at(u)
                if t == 0:
                    half = q // HALF
                    pe.wait_ge(s_stk[0][half], 32 * (b + 1))
                    pe.wait_ge(s_stk[2][half], 32 * (b + 1))
                wait(pe, s_ttr, NT * u + t - 1)
                pe.matmul(ps_con[:, t % 2, :], QU[rows, q, t * P:(t + 1) * P], KK[rows, q, :],
                          start=True, stop=True).then_inc(s_con, 1)

            def turn(u, j):
                if j == 0:
                    pe.wait_ge(s_exp, NT * (u + 1))
                wait(pe, s_te, NT * u + j - 1)
                for t in range(NT):
                    last = pe.transpose(ps_pt[:, j % 2, t * P:(t + 1) * P],
                                        sc_sb[:, u % N_SC, t, j * P:(j + 1) * P], id_sb[:, :])
                last.then_inc(s_pt, 1)

            def values(u, j):
                b, h = u // H, u % H
                if j == 0:
                    if h == 0:
                        pe.wait_ge(s_jev, job("V", b))
                    if h % 4 == 0:
                        wait(pe, s_oev, u // 4)
                pe.wait_ge(s_te, NT * u + j + 1)
                for t in range(NT):
                    last = pe.matmul(ps_av[32 * t:32 * t + 2 * DH, h % 4, :], v_sb[:, b % 2, j, h, :],
                                     pt_sb[:, (NT * u + j) % N_PT, t * P:(t + 1) * P],
                                     start=(j == 0), stop=(j == NT - 1))
                last.then_inc(s_av, 1)

            for n in STEPS:
                u, m, p = unit(n, 0), unit(n, CONTENT_LAG), unit(n, TURN_LAG)
                for t in range(NT):
                    if u is not None:
                        positions(u, t)
                    if m is not None:
                        content(m, t)
                    if p is not None:
                        turn(p, t)
                    q = NT * (n - TURN_LAG) + t - VALUES_LAG
                    if 0 <= q < NT * UNITS:
                        values(q // NT, q % NT)
                    if t < JOB_PARTS:
                        for j in jobs(n):
                            do_job(*j, t)


JOB_PARTS = 3
N_SMALL = 21
BIG = 3.4e38


def kernel(**inputs):
    import numpy as np
    import concourse.bacc as bacc
    from concourse.bass_utils import run_bass_kernel_spmd

    D, S, H, DH = 128, 512, 16, 8

    def perm(a):
        a = np.asarray(a)
        lead = a.shape[:-1]
        return np.ascontiguousarray(
            np.moveaxis(a.reshape(*lead, H // 2, 2, DH), -3, -1).reshape(*lead, D))

    pos = np.arange(S, dtype=np.float32)[:, None]
    div = np.exp(np.arange(0, D, 2, dtype=np.float32) * np.float32(-np.log(10000.0) / D)).astype(np.float32)
    ang = (pos * div).astype(np.float32)
    pe = np.stack([np.sin(ang), np.cos(ang)], axis=-1).reshape(S, D).astype(np.float32)

    g = {k[3:]: np.asarray(v) for k, v in inputs.items()}
    data = {
        "x": g["attn_x"], "ln_g": g["attn_ln_g"], "ln_b": g["attn_ln_b"],
        "wq": perm(g["attn_Wq"]), "bq": perm(g["attn_bq"]), "wk": perm(g["attn_Wk"]), "bk": perm(g["attn_bk"]),
        "wv": g["attn_Wv"], "bv": g["attn_bv"], "wp": perm(g["attn_Wp"]), "wo": g["attn_Wo"], "bo": g["attn_bo"],
        "u_bias": perm(g["attn_u_bias"].reshape(D)), "v_bias": perm(g["attn_v_bias"].reshape(D)),
        "k0": g["ffn_k0"], "k1": g["ffn_k1"], "k2": g["ffn_k2"],
        "s0": g["ffn_s0"].reshape(1), "s1": g["ffn_s1"].reshape(1), "s2": g["ffn_s2"].reshape(1),
        "pe_t": np.ascontiguousarray(pe.T), "ident": np.eye(D, dtype=np.float32),
    }
    nc = bacc.Bacc("TRN2", target_bir_lowering=False, num_devices=1)
    arrays, args = {}, []
    for name, a in data.items():
        a = np.ascontiguousarray(a)
        arrays[f"in_{name}"] = a
        args.append(nc.dram_tensor(f"in_{name}", a.shape, mybir.dt.from_np(a.dtype), kind="ExternalInput").ap())
    out = nc.dram_tensor("out", g["attn_x"].shape, F32, kind="ExternalOutput").ap()
    attention_mlp(nc, *args, out)
    r = run_bass_kernel_spmd(nc, [arrays], core_ids=[0])
    return r.results[0]["out"]
```

```python
from contextlib import ExitStack

import concourse.bass as bass
from concourse import mybir

ALU = mybir.AluOpType
ACT = mybir.ActivationFunctionType
F32 = mybir.dt.float32
BF16 = mybir.dt.bfloat16
F32R = mybir.dt.float32r
U8 = mybir.dt.uint8

P = 128
EPS = 1e-5
Q_RUNS = ((0, 3), (0, 2), (0, 1))
K_RUNS = ((0, 3), (1, 2), (2, 1))
NR = 6


def attention_mlp(nc, x, consts, wp, pe_t, k0, k1, k2, out):
    B, S, D = x.shape
    H, DH = 16, 8
    assert D == P and H * DH == P and S == 512 and k0.shape[1] == S
    NT = S // P
    UNITS = B * H
    PAIRS = H // 2
    BIAS = NR * DH
    KR = BIAS + 3
    HALF = PAIRS // 2
    F1, F2 = k0.shape[1], k1.shape[1]
    C1, C2 = F1 // P, F2 // P
    SCALE = float(DH) ** -0.5
    PITCH = S + 1

    SHIFT_LAG = 2
    CONTENT_LAG = 4
    TURN_Q = NT * CONTENT_LAG + 6
    VALUES_Q = TURN_Q + 2
    HEADS_SLOT = -(-VALUES_Q // NT)
    N_X = 4
    N_POS = 3
    N_SC = 5
    N_SHIFT = 6
    N_PT = 4

    shift = nc.dram_tensor("shift", [N_SHIFT, S * PITCH], F32, kind="Internal").ap()
    pcs = [nc.dram_tensor(f"pieces_{n}", [2, 3, DH * PAIRS, S], BF16, kind="Internal").ap()
           for n in ("q", "k", "p")]
    pcs_b = [nc.dram_tensor(f"pieces_{n}", [3, 2, PAIRS, S], BF16, kind="Internal").ap() for n in ("uk", "vp")]
    heads_d = nc.dram_tensor("heads_d", [P, NT, P], F32, kind="Internal").ap()

    with ExitStack() as ctx:
        def sb(name, shape, dt=F32):
            return ctx.enter_context(nc.sbuf_tensor(name, shape, dt))

        def psum(name, shape):
            return ctx.enter_context(nc.psum_tensor(name, shape, F32))

        def sem(name):
            return ctx.enter_context(nc.semaphore(name))

        c_sb = sb("c_sb", [P, P + H + 10 + 5 * D])
        at = [0]

        def const(width):
            at[0] += width
            return c_sb[:, at[0] - width:at[0]]

        id_sb = const(P)
        by_head = const(H)
        cols = const(10)
        G, BB, BQ, BK, UB, VB, BO, _, _, S2 = (cols[:, i:i + 1] for i in range(10))
        bv_row = const(D)
        w_sb = {n: const(D) for n in ("q", "k", "v", "o")}
        assert at[0] == consts.shape[1]
        col2 = sb("col2", [P, 2])
        u_mat = sb("u_mat", [P, H])
        v_mat = sb("v_mat", [P, H])
        w0 = sb("w0", [P, F1], F32R)
        w1 = sb("w1", [P, C1, F2], F32R)
        w2 = sb("w2", [P, C2, D], F32R)
        half_pow = sb("half_pow", [P, NT])

        x_sb = sb("x_sb", [P, N_X, NT, D])
        x1_sb = sb("x1_sb", [P, NT, D])
        z_sb = sb("z_sb", [P, NT, D])
        stats = sb("stats", [P, 2, NT, 6])
        mv = sb("mv", [P, 2, NT, 2])
        var_eps = sb("var_eps", [P, 2, NT])
        rstd = sb("rstd", [P, 2, NT])
        x1_t = sb("x1_t", [P, 2, 2, S], F32R)
        z_t = sb("z_t", [P, S])
        full = [sb("full_q", [P, S]), sb("full_k", [P, S]), sb("full_uk", [H, S])]
        pe_sb = full[1]
        rest = sb("rest", [P, S])
        piece = [sb("pieces_sb_q", [P, 3, S], BF16), sb("pieces_sb_k", [P, 3, S], BF16),
                 sb("pieces_sb_uk", [H, 3, S], BF16)]
        stack = [sb(f"stack_{n}", [P, PAIRS, S], BF16) for n in ("q", "k", "p")]
        QQ, KK, PP = stack
        v_sb = sb("v_sb", [P, 2, NT, H, DH])

        pos_sb = sb("pos_sb", [P, N_POS, NT, PITCH])
        sc_sb = sb("sc_sb", [P, N_SC, NT, S])
        nmax = sb("nmax", [P, N_SC, NT])
        pt_sb = sb("pt_sb", [P, N_PT, S])
        o_sb = sb("o_sb", [P, H, P])
        o_t = sb("o_t", [P, S])
        sums = sb("sums", [P, 2, NT, H])
        inv = sb("inv", [P, NT, H])
        inv_dims = sb("inv_dims", [P, NT, DH, H])

        stage = pt_sb[:, :, :].rearrange("p a c -> p (a c)").bitcast(U8)
        k0_u8 = stage[:, 0:2 * F1].rearrange("p (a n) -> p a n", a=2)
        k1_u8 = stage[:, 2 * F1:2 * F1 + C1 * F2].rearrange("p (a n) -> p a n", a=C1)
        k2_u8 = stage[:, 2 * F1 + C1 * F2:2 * F1 + C1 * F2 + C2 * D].rearrange("p (a n) -> p a n", a=C2)
        act_sb = sb("act_sb", [P, 2, S])
        w_sb["p"] = act_sb[:, 0, 0:D]
        h1 = sb("h1", [P, C1, 2, S], F32R)
        h2 = sb("h2", [P, C2, 2, S], F32R)
        y_t = sb("y_t", [P, S])

        ps_pos = psum("ps_pos", [P, 2, S])
        ps_con = psum("ps_con", [P, 2, S])
        ps_pt = psum("ps_pt", [P, 2, S])
        ps_av = psum("ps_av", [P, 4, P])
        ps_job = psum("ps_job", [P, S])

        s_w = sem("s_w")
        s_wb = sem("s_wb")
        s_ones = sem("s_ones")
        s_wf = sem("s_wf")
        s_x = [sem(f"s_x{i}") for i in range(N_X)]
        s_chain = sem("s_chain")
        s_pool = sem("s_pool")
        s_st1, s_st2 = sem("s_st1"), sem("s_st2")
        s_rstd = sem("s_rstd")
        s_x1, s_z = sem("s_x1n"), sem("s_z")
        s_job = sem("s_job")
        s_jev = sem("s_jev")
        s_split = sem("s_split")
        s_pw = [sem(f"s_pw{i}") for i in range(3)]
        s_stk = [[sem(f"s_stk{i}{j}") for j in range(2)] for i in range(3)]
        s_pos, s_con, s_pt, s_av = sem("s_pos"), sem("s_con"), sem("s_pt"), sem("s_av")
        s_pe = sem("s_pe")
        s_out_w = [sem(f"s_pout{i}") for i in range(N_POS)]
        s_in = [sem(f"s_in{i}") for i in range(N_SC)]
        s_ttr, s_exp = sem("s_ttr"), sem("s_exp")
        s_te = sem("s_te")
        s_oev = sem("s_oev")
        s_hw, s_hr = sem("s_hw"), sem("s_hr")
        s_inv = sem("s_inv")
        s_invd = sem("s_invd")
        s_out = sem("s_out")
        s_hl = sem("s_hl")

        ONES = 8

        def wait(eng, s, n):
            if n > 0:
                eng.wait_ge(s, n)

        SLOT = {}
        order = []

        def add(step, name, b, c=0):
            SLOT.setdefault(step, []).append((name, b, c))

        LAST = ((8, "INV", 0), (10, "WO", 0), (11, "TY", 0))
        THIS = ((0, "L1", 0), (3, "L1", 1), (6, "L1", 2), (9, "L1", 3), (12, "L2", 0))
        FIRST = ((0, "L0", 0), (0, "L0", 1), (1, "L0", 2), (2, "L0", 3),
                 (3, "L1", 0), (6, "L1", 1), (8, "L1", 2), (9, "L1", 3), (12, "L2", 0))
        NEXT = ((1, "T1", 0), (2, "TZ", 0), (4, "Q", 0), (5, "K", 0), (7, "UK", 0),
                (10, "L0", 0), (11, "L0", 1), (13, "L0", 2), (14, "L0", 3), (15, "V", 0))
        for it in range(-1, B + 1):
            if it == -1:
                add(-16, "P", 0)
                add(-16, "VP", 0)
            for b, todo in ((it - 1, LAST), (it, THIS if it else FIRST), (it + 1, NEXT)):
                for slot, name, c in todo if 0 <= b < B else ():
                    if (name, b) != ("L0", 0) or it == 0:
                        add(16 * it + slot, name, b, c)
        STATS_SLOTS, NORM_SLOTS = (1, 10), (2, 12)
        STEPS = range(-16, 16 * B + 16)
        for n in STEPS:
            order += SLOT.get(n, [])
        JOB = {j: i + 1 for i, j in enumerate(order)}

        def jobs(n):
            return SLOT.get(n, [])

        def taken(n, t):
            todo = jobs(n)
            every = NT // max(1, len(todo))
            return [j for i, j in enumerate(todo) if t == every * (i + 1) - 1]

        def parts(n, t):
            todo = jobs(n)
            if len(todo) == 1:
                return [(todo[0], t, NT - 1)] if t < NT - 1 else []
            every = NT // max(1, len(todo))
            return [(j, 0, 1) for i, j in enumerate(todo) if t == every * i]

        def job(name, b, c=0):
            return JOB[(name, b, c)] if b >= 0 else 0

        SPLIT = {(0, -1): 0, (2, -1): 1}
        for b in range(B):
            for i in range(3):
                SPLIT[(i, b)] = len(SPLIT)
        PIECES_OUT = {(i, b): 16 * (2, 2, 1)[i] * (b + 1 + (i != 1)) for i in range(3) for b in range(-1, B)}

        ACTS = {}
        for j in order:
            if j[0] in ("T1", "L0", "L1"):
                ACTS[j] = len(ACTS)

        STACK_IN = [16 * 2 * len(Q_RUNS), 16 * 2 * (len(K_RUNS) + 1), 16 * 2 * (len(K_RUNS) + 1)]

        def two(name, b, c):
            return {"T1": x1_t[:, b % 2], "L0": h1[:, c], "L1": h2[:, c]}[name]

        def multiplied(name, b, c):
            return {"T1": job("L0", b - 2, C1 - 1), "L0": job("L1", b - 1, C2 - 1), "L1": job("L2", b - 1)}[name]

        def block_of(n, t, lag):
            q = NT * n + t - lag
            return divmod(q, NT) if 0 <= q < NT * UNITS else (None, None)

        def unit(n, lag):
            return n - lag if 0 <= n - lag < UNITS else None

        def scale_rows(eng, b, k):
            src, dst = ((x_sb[:, b % N_X], x1_sb), (x1_sb, z_sb))[k]
            for t in range(NT):
                last = eng.tensor_scalar(dst[:, t, :], src[:, t, :], mv[:, k, t, 0:1], rstd[:, k, t:t + 1],
                                         ALU.subtract, ALU.mult)
            last.then_inc((s_x1, s_z)[k], 1)

        def split(eng, own, i, b, ready):
            src, pc = full[i][:, :], piece[i]
            high, mid, low = (pc[:, n, :] for n in ((0, 1, 2) if (i, b >= 0) == (0, True) else (2, 1, 0)))
            left = rest[0:H, :] if i == 2 else rest[:, :]
            wait(eng, s_split, SPLIT[(i, b)])
            if b >= 0:
                wait(eng, s_pw[i], PIECES_OUT[(i, b - 1)])
            eng.wait_ge(s_jev, ready)
            own(eng.tensor_copy(high, src))
            eng.tensor_tensor(left, src, high, ALU.subtract)
            own(eng.tensor_tensor(mid, src, high, ALU.subtract))
            eng.tensor_tensor(low, left, mid, ALU.subtract).then_inc(s_split, 1)

        block = ctx.enter_context(nc.Block())

        @block.sync
        def _(sp):
            def load_x(b):
                wait(sp, s_out, 16 * (b - N_X + 1))
                sp.dma_start(x_sb[:, b % N_X], x[b].rearrange("(p t) d -> p t d", t=NT)) \
                  .then_inc(s_x[b % N_X], 16)

            load_x(0)
            for dst, src in ((c_sb[:, :], consts), (w_sb["p"], wp), (pe_sb[:, :], pe_t)):
                sp.dma_start(dst, src).then_inc(s_w, 16)
            for dst, src in ((k0_u8, k0), (k1_u8, k1), (k2_u8, k2)):
                sp.dma_start(dst, src.rearrange("(a p) n -> p a n", p=P)).then_inc(s_wb, 16)
            load_x(1)

            def write_pieces(i, b, dst):
                wait(sp, s_split, SPLIT[(i, b)] + 1)
                if i == 2:
                    sp.dma_start(dst.rearrange("r a q c -> (a q) r c"), piece[2][:, :, :]).then_inc(s_pw[2], 16)
                else:
                    for par in range(2):
                        sp.dma_start(dst[par].rearrange("r q c -> q r c"),
                                     piece[i][64 * par:64 * par + 64, :, :]).then_inc(s_pw[i], 16)

            def read_stack(j, b, half, part=0, parts=1):
                q = slice(HALF * half, HALF * half + HALF)
                todo = []
                for par in range(2):
                    row = 64 * par
                    for first, many in (Q_RUNS, K_RUNS, K_RUNS)[j]:
                        rows = pcs[j][par, first:first + many].rearrange("r (d q) c -> (r d) q c", q=PAIRS)
                        todo.append((row, DH * many, rows[:, q, :], j % 2))
                        row += DH * many
                for par in range(2 if j else 0):
                    todo.append((64 * par + BIAS, 3, (None, pcs_b[0], pcs_b[1])[j][:, par, q, :], 2))
                for i in range(part, len(todo), parts):
                    row, many, src, buf = todo[i]
                    sp.wait_ge(s_pw[buf], PIECES_OUT[(buf, b)])
                    sp.dma_start(stack[j][row:row + many, q, :], src).then_inc(s_stk[j][half], 16)

            late = CONTENT_LAG
            FILLS = (((late, late + 1), 0, 1, 0, 0), ((7, 8, 9, 10), 1, 1, 0, 0),
                     ((late + 8, late + 9, late + 10), 0, 0, 1, 8),
                     ((late + 11, late + 12, late + 13, late + 14), 1, 0, 1, 8))

            for n in STEPS:
                it, slot = n // 16, n % 16
                if it == -1 and slot == 1:
                    sp.wait_ge(s_ones, ONES)
                    write_pieces(0, -1, pcs[2])
                    write_pieces(2, -1, pcs_b[1])
                    read_stack(2, -1, 0)
                if it >= 1 and slot == 12:
                    wait(sp, s_jev, job("TY", it - 1))
                    sp.dma_start(out[it - 1].rearrange("(p t) d -> p t d", t=NT),
                                 x_sb[:, (it - 1) % N_X]).then_inc(s_out, 16)
                if it == 0 and slot in (1, 2):
                    read_stack(2, -1, 1, slot - 1, 2)
                for slots, j, half, ahead, used in FILLS:
                    for part, at in enumerate(slots):
                        b = (n - at) // 16 + ahead
                        if (n - at) % 16 == 0 and 0 <= b < B:
                            wait(sp, s_con, NT * (16 * (b - ahead) + used))
                            read_stack(j, b, half, part, len(slots))
                for i, dst, at in ((0, pcs[0], 11), (1, pcs[1], 14), (2, pcs_b[0], 14)):
                    if it + 1 < B and slot == at:
                        for half in range(2):
                            wait(sp, s_stk[min(i, 1)][half], STACK_IN[min(i, 1)] * (it + 1))
                        write_pieces(i, it + 1, dst)
                if it >= 1 and slot == HEADS_SLOT:
                    sp.wait_ge(s_oev, 4 * it)
                    for t in range(NT):
                        sp.dma_start(heads_d[:, t, :].rearrange("(d h) c -> d h c", h=H),
                                     o_sb[32 * t:32 * t + DH, :, :]).then_inc(s_hw, 16)
                if it >= 1 and slot == HEADS_SLOT + 1:
                    sp.wait_ge(s_hw, 16 * NT * it)
                    wait(sp, s_job, job("WO", it - 2))
                    sp.dma_start(o_t[:, :], heads_d.rearrange("p t c -> p (t c)")).then_inc(s_hr, 16)
                if 2 <= it + 3 < B and slot == 15:
                    load_x(it + 3)
                u = unit(n, SHIFT_LAG)
                if u is not None:
                    sp.wait_ge(s_out_w[u % N_POS], 16 * (u // N_POS + 1))
                    wait(sp, s_pt, NT * (u - N_SC + 1))
                    sp.dma_start(sc_sb[:, u % N_SC].rearrange("p t c -> p (t c)"),
                                 shift[u % N_SHIFT, S - 1:S - 1 + S * S].rearrange("(p c) -> p c", p=P)) \
                      .then_inc(s_in[u % N_SC], 16)
                u = unit(n, 0)
                if u is not None:
                    sp.wait_ge(s_pe, NT * (u + 1))
                    if u >= N_SHIFT:
                        v = u - N_SHIFT
                        sp.wait_ge(s_in[v % N_SC], 16 * (v // N_SC + 1))
                    sp.dma_start(shift[u % N_SHIFT].rearrange("(p c) -> p c", p=P),
                                 pos_sb[:, u % N_POS].rearrange("p t c -> p (t c)")) \
                      .then_inc(s_out_w[u % N_POS], 16)
            sp.wait_ge(s_out, 16 * B)

        @block.gpsimd
        def _(pool):
            done = [0]

            def own(ins):
                done[0] += 1
                ins.then_inc(s_pool, 1)
                pool.wait_ge(s_pool, done[0])

            pool.memset(half_pow[:, :], -0.5).then_inc(s_ones, 1)
            pool.memset(pos_sb[:, :, :, S:PITCH], 0.0).then_inc(s_ones, 1)
            pool.memset(QQ[:, :, :], 1.0).then_inc(s_ones, 1)

            def norm(b, k):
                pool.wait_ge((s_st1, s_st2)[k], b + 1)
                own(pool.tensor_scalar(var_eps[:, k, :], mv[:, k, :, 1], EPS, None, ALU.add))
                own(pool.tensor_tensor(rstd[:, k, :], var_eps[:, k, :], half_pow[:, :], ALU.pow))
                if b == 0:
                    pool.sem_inc(s_rstd, 1)
                else:
                    wait(pool, s_job, job(("T1", "TZ")[k], b - 1))
                    scale_rows(pool, b, k)

            def split2(name, b, c):
                k, dst = ACTS[(name, b, c)], two(name, b, c)
                pool.wait_ge(s_jev, job(name, b, c))
                wait(pool, s_job, multiplied(name, b, c))
                own(pool.tensor_copy(dst[:, 0, :], act_sb[:, k % 2, :]))
                pool.tensor_tensor(dst[:, 1, :], act_sb[:, k % 2, :], dst[:, 0, :].bitcast(F32), ALU.subtract) \
                    .then_inc(s_hl, 1)

            norm(0, 0)
            norm(0, 1)
            pool.wait_ge(s_ones, ONES)
            for n in STEPS:
                it, slot = n // 16, n % 16
                for name, b, c in jobs(n):
                    if name in ("T1", "L0", "L1"):
                        split2(name, b, c)
                    elif name in ("Q", "K", "UK") and b > 0:
                        split(pool, own, ("Q", "K", "UK").index(name), b, job(name, b))
                if it >= 1 and slot == CONTENT_LAG + 1:
                    pool.wait_ge(s_inv, it)
                    wait(pool, s_job, job("INV", it - 2))
                    pool.tensor_copy(inv_dims[:, :, :, :],
                                     inv[:, :, :].unsqueeze(2).broadcast_to([P, NT, DH, H])).then_inc(s_invd, 1)
                if it + 2 < B and slot in NORM_SLOTS:
                    norm(it + 2, NORM_SLOTS.index(slot))

        @block.scalar
        def _(act):
            act.wait_ge(s_w, 16 * N_WEIGHTS)
            act.wait_ge(s_ones, ONES)

            def take_job(name, b, c):
                k = job(name, b, c)
                act.wait_ge(s_job, k)
                if name == "P":
                    last = act.copy(full[0][:, :], ps_job[:, :])
                elif name in ("VP", "UK"):
                    if name == "UK":
                        wait(act, s_split, SPLIT[(2, b - 1)] + 1)
                    last = act.copy(full[2][:, :], ps_job[0:H, :])
                elif name == "T1":
                    wait(act, s_hl, ACTS[(name, b, c)] - 1)
                    last = act.copy(act_sb[:, ACTS[(name, b, c)] % 2, :], ps_job[:, :])
                elif name == "TZ":
                    last = act.activation(z_t[:, :].rearrange("d (p t) -> d t p", t=NT),
                                          ps_job[:, :].rearrange("d (t p) -> d t p", t=NT),
                                          ACT.Identity, bias=BB, scale=G)
                elif name in ("Q", "K"):
                    i = ("Q", "K").index(name)
                    wait(act, s_split, SPLIT[(i, b - 1)] + 1 if b or i == 0 else 1)
                    last = act.activation(full[i][:, :], ps_job[:, :], ACT.Identity, bias=(BQ, BK)[i], scale=1.0)
                elif name in ("L0", "L1"):
                    wait(act, s_hl, ACTS[(name, b, c)] - 1)
                    k = ("L0", "L1").index(name)
                    last = act.activation(act_sb[:, ACTS[(name, b, c)] % 2, :], ps_job[:, :], ACT.Relu,
                                          scale=col2[:, k:k + 1])
                elif name == "L2":
                    wait(act, s_job, job("TY", b - 1))
                    last = act.activation(y_t[:, :], ps_job[:, :], ACT.Identity, bias=BO, scale=S2)
                else:
                    return
                last.then_inc(s_jev, 1)

            for n in STEPS:
                u, m = unit(n, 0), unit(n, CONTENT_LAG)
                for t in range(NT):
                    if u is not None:
                        act.wait_ge(s_pos, NT * u + t + 1)
                        if t == 0 and u >= N_POS:
                            act.wait_ge(s_out_w[u % N_POS], 16 * (u // N_POS))
                        act.copy(pos_sb[:, u % N_POS, t, 0:S], ps_pos[:, t % 2, :]).then_inc(s_pe, 1)
                    if m is not None:
                        act.wait_ge(s_ttr, NT * m + t + 1)
                        b, h = divmod(m, H)
                        wait(act, s_inv, b - 1)
                        act.activation(sc_sb[:, m % N_SC, t, :], sc_sb[:, m % N_SC, t, :], ACT.Exp,
                                       bias=nmax[:, m % N_SC, t:t + 1], scale=-1.0,
                                       accum_out=sums[:, b % 2, t, h:h + 1]).then_inc(s_exp, 1)
                    for j in taken(n, t):
                        take_job(*j)

        @block.vector
        def _(dve):
            done = [0]

            def own(ins):
                done[0] += 1
                ins.then_inc(s_chain, 1)
                dve.wait_ge(s_chain, done[0])

            dve.memset(ps_av[:, :, :], 0.0).then_inc(s_ones, 1)
            dve.memset(nmax[:, :, :], 0.0).then_inc(s_ones, 1)

            def norm_stats(b, k):
                src = (x_sb[:, b % N_X], x1_sb[:, :, :])[k]
                if k == 0:
                    dve.wait_ge(s_x[b % N_X], 16 * (b // N_X + 1))
                    wait(dve, s_x1, b)
                else:
                    dve.wait_ge(s_x1, b + 1)
                    wait(dve, s_z, b)
                for t in range(NT):
                    last = dve.bn_stats(stats[:, k, t, :], src[:, t, :])
                own(last)
                for t in range(NT):
                    last = dve.bn_aggr(mv[:, k, t, :], stats[:, k, t, :])
                last.then_inc((s_st1, s_st2)[k], 1)

            def take_job(name, b, c):
                k = job(name, b, c)
                if name in ("P", "VP") or name in ("Q", "K", "UK") and b == 0:
                    i, to = {"P": (0, -1), "VP": (2, -1), "Q": (0, 0), "K": (1, 0), "UK": (2, 0)}[name]
                    split(dve, own, i, to, k)
                if name not in ("V", "INV", "WO", "TY"):
                    return
                dve.wait_ge(s_job, k)
                if name == "V":
                    wait(dve, s_av, NT * H * (b - 1))
                    last = dve.tensor_tensor(
                        v_sb[:, b % 2],
                        ps_job[:, :].rearrange("p (j h d) -> p j h d", j=NT, d=DH),
                        bv_row.rearrange("p (h d) -> p h d", d=DH).unsqueeze(1)
                        .broadcast_to([P, NT, H, DH]), ALU.add)
                elif name == "INV":
                    dve.wait_ge(s_hr, 16 * (b + 1))
                    last = dve.tensor_tensor(o_t[:, :], o_t[:, :], ps_job[:, :], ALU.mult)
                elif name == "WO":
                    last = dve.tensor_tensor(y_t[:, :], ps_job[:, :], y_t[:, :], ALU.add)
                else:
                    x_out = x_sb[:, b % N_X].rearrange("p t c -> p (t c)")
                    last = dve.tensor_tensor(x_out, ps_job[:, :], x_out, ALU.add)
                last.then_inc(s_jev, 1)

            for k in range(2):
                norm_stats(0, k)
                dve.wait_ge(s_rstd, k + 1)
                scale_rows(dve, 0, k)
                if k == 0:
                    dve.wait_ge(s_w, 16 * N_WEIGHTS)
                    dve.tensor_scalar(u_mat[:, :], by_head, UB, None, ALU.mult).then_inc(s_ones, 1)
                    dve.tensor_scalar(v_mat[:, :], by_head, VB, None, ALU.mult).then_inc(s_ones, 1)
                    dve.tensor_scalar(col2[:, 0:2], cols[:, 7:9], 2.0, None, ALU.mult).then_inc(s_ones, 1)
            dve.wait_ge(s_wb, 16 * 3)
            half0 = y_t[:, :]
            dve.tensor_scalar(w0[:, :], k0_u8[:, 0, :], 2.0, None, ALU.mult)
            own(dve.tensor_scalar(half0, k0_u8[:, 1, :], 2.0, None, ALU.mult))
            dve.tensor_tensor(w0[:, :], w0[:, :].bitcast(F32), half0, ALU.subtract)
            dve.tensor_scalar(w1[:, :, :], k1_u8, 2.0, -1.0, ALU.mult, ALU.add)
            own(dve.tensor_scalar(w2[:, :, :], k2_u8, 2.0, -1.0, ALU.mult, ALU.add))
            dve.sem_inc(s_wf, 1)
            for n in STEPS:
                it, slot = n // 16, n % 16
                m = unit(n, CONTENT_LAG)
                for t in range(NT):
                    if m is not None:
                        dve.wait_ge(s_con, NT * m + t + 1)
                        if t == 0:
                            dve.wait_ge(s_in[m % N_SC], 16 * (m // N_SC + 1))
                        dve.tensor_tensor_reduce(sc_sb[:, m % N_SC, t, :], ps_con[:, t % 2, :],
                                                 sc_sb[:, m % N_SC, t, :], -SCALE, BIG, ALU.add, ALU.min,
                                                 nmax[:, m % N_SC, t:t + 1]).then_inc(s_ttr, 1)
                    p, j = block_of(n, t, TURN_Q)
                    if p is not None:
                        q = NT * p + j
                        dve.wait_ge(s_pt, q + 1)
                        if q == 0:
                            dve.wait_ge(s_wf, 1)
                        wait(dve, s_av, q - N_PT + 1)
                        dve.tensor_copy(pt_sb[:, q % N_PT], ps_pt[:, j % 2, :]).then_inc(s_te, 1)
                    o, j = block_of(n, t, VALUES_Q)
                    if j == NT - 1 and o % 4 == 3:
                        dve.wait_ge(s_av, NT * (o + 1))
                        wait(dve, s_hw, 16 * NT * (o // H))
                        dve.tensor_copy(o_sb[:, o % H - 3:o % H + 1, :], ps_av[:, :, :]).then_inc(s_oev, 1)
                    if it >= 1 and slot == CONTENT_LAG + 1 and t == 0:
                        dve.wait_ge(s_exp, NT * H * it)
                        wait(dve, s_invd, it - 1)
                        dve.reciprocal(inv[:, :, :], sums[:, (it - 1) % 2]).then_inc(s_inv, 1)
                    for j in taken(n, t):
                        take_job(*j)
                if it + 2 < B and slot in STATS_SLOTS:
                    norm_stats(it + 2, STATS_SLOTS.index(slot))

        @block.tensor
        def _(pe):
            pe.wait_ge(s_w, 16 * N_WEIGHTS)
            pe.wait_ge(s_ones, ONES)

            def job_parts(name, b, c):
                if name == "P":
                    return [lambda: pe.matmul(ps_job[:, :], w_sb["p"], pe_sb[:, :], start=True, stop=True)]
                if name in ("VP", "UK"):
                    mat, src = (v_mat, full[0]) if name == "VP" else (u_mat, full[1])
                    return [lambda: pe.matmul(ps_job[0:H, :], mat[:, :], src[:, :], start=True, stop=True)]
                if name == "Q":
                    return [lambda: pe.matmul(ps_job[:, :], w_sb["q"],
                                              z_t[:, :].rearrange("d (p t) -> d t p", t=NT), start=True, stop=True)]
                if name == "K":
                    return [lambda: pe.matmul(ps_job[:, :], w_sb["k"], z_t[:, :], start=True, stop=True)]
                if name == "WO":
                    return [lambda: pe.matmul(ps_job[:, :], w_sb["o"], o_t[:, :], start=True, stop=True)]
                if name == "INV":
                    def inverse(t):
                        if t == 0:
                            pe.wait_ge(s_invd, b + 1)
                        return pe.matmul(ps_job[:, t * P:(t + 1) * P],
                                         inv_dims[:, t].rearrange("p d h -> p (d h)"), id_sb,
                                         start=True, stop=True)
                    return [lambda t=t: inverse(t) for t in range(NT)]
                if name in ("T1", "TZ", "V", "TY"):
                    def block(t):
                        dst, cut = ps_job[:, t * P:(t + 1) * P], slice(t * P, (t + 1) * P)
                        if name == "V":
                            return pe.matmul(dst, z_t[:, cut], w_sb["v"], start=True, stop=True)
                        if name == "TY":
                            return pe.transpose(dst, y_t[:, cut], id_sb)
                        src, ready = ((x1_sb, s_x1), (z_sb, s_z))[name == "TZ"]
                        if t == 0:
                            pe.wait_ge(ready, b + 1)
                        return pe.transpose(dst, src[:, t, :], id_sb)
                    return [lambda t=t: block(t) for t in range(NT)]
                w, src, before = {"L0": (w0, x1_t[:, b % 2].unsqueeze(1), [("T1", b, 0)]),
                                  "L1": (w1, h1, [("L0", b, a) for a in range(C1)]),
                                  "L2": (w2, h2, [("L1", b, a) for a in range(C2)])}[name]

                def product(a, hl):
                    if name == "L0" and b == 0 and c == 0:
                        pe.wait_ge(s_wf, 1)
                    if hl == 0:
                        pe.wait_ge(s_hl, ACTS[before[a]] + 1)
                    lhs = w[:, c * P:(c + 1) * P] if name == "L0" else w[:, a, c * P:(c + 1) * P]
                    return pe.matmul(ps_job[:, :], lhs, src[:, a, hl, :],
                                     start=(a == 0 and hl == 0), stop=(a == len(before) - 1 and hl == 1))
                return [lambda a=a, hl=hl: product(a, hl) for a in range(len(before)) for hl in range(2)]

            def do_job(name, b, c, part, many):
                k, todo = job(name, b, c), job_parts(name, b, c)
                first, end = (-(-len(todo) * i // many) for i in (part, part + 1))
                if part == 0:
                    wait(pe, s_jev, k - 1)
                for i in range(first, end):
                    last = todo[i]()
                if first < end == len(todo):
                    last.then_inc(s_job, 1)

            def at(u):
                h = u % H
                base = 64 * (h % 2)
                return slice(base, base + KR), h // 2

            def positions(u, t):
                b, (rows, q) = u // H, at(u)
                if t == 0:
                    half = q // HALF
                    pe.wait_ge(s_stk[2][half], STACK_IN[2])
                    pe.wait_ge(s_stk[0][half], STACK_IN[0] * (b + 1))
                wait(pe, s_pe, NT * u + t - 1)
                pe.matmul(ps_pos[:, t % 2, :], QQ[rows, q, t * P:(t + 1) * P], PP[rows, q, :],
                          start=True, stop=True).then_inc(s_pos, 1)

            def content(u, t):
                b, (rows, q) = u // H, at(u)
                if t == 0:
                    half = q // HALF
                    pe.wait_ge(s_stk[1][half], STACK_IN[1] * (b + 1))
                wait(pe, s_ttr, NT * u + t - 1)
                pe.matmul(ps_con[:, t % 2, :], QQ[rows, q, t * P:(t + 1) * P], KK[rows, q, :],
                          start=True, stop=True).then_inc(s_con, 1)

            def turn(u, j):
                if j == 0:
                    pe.wait_ge(s_exp, NT * (u + 1))
                wait(pe, s_te, NT * u + j - 1)
                for t in range(NT):
                    last = pe.transpose(ps_pt[:, j % 2, t * P:(t + 1) * P],
                                        sc_sb[:, u % N_SC, t, j * P:(j + 1) * P], id_sb)
                last.then_inc(s_pt, 1)

            def values(u, j):
                b, h = u // H, u % H
                if j == 0:
                    if h == 0:
                        pe.wait_ge(s_jev, job("V", b))
                    if h % 4 == 0:
                        wait(pe, s_oev, u // 4)
                pe.wait_ge(s_te, NT * u + j + 1)
                for t in range(NT):
                    last = pe.matmul(ps_av[32 * t:32 * t + DH, h % 4, :], v_sb[:, b % 2, j, h, :],
                                     pt_sb[:, (NT * u + j) % N_PT, t * P:(t + 1) * P],
                                     start=(j == 0), stop=(j == NT - 1))
                last.then_inc(s_av, 1)

            for n in STEPS:
                u, m = unit(n, 0), unit(n, CONTENT_LAG)
                for t in range(NT):
                    if u is not None:
                        positions(u, t)
                    if m is not None:
                        content(m, t)
                    p, j = block_of(n, t, TURN_Q)
                    if p is not None:
                        turn(p, j)
                    o, j = block_of(n, t, VALUES_Q)
                    if o is not None:
                        values(o, j)
                    for j, part, many in parts(n, t):
                        do_job(*j, part, many)


N_WEIGHTS = 3
BIG = 3.4e38


def kernel(**inputs):
    import numpy as np
    import concourse.bacc as bacc
    from concourse.bass_utils import run_bass_kernel_spmd

    D, S, H, DH = 128, 512, 16, 8

    def perm(a):
        a = np.asarray(a)
        lead = a.shape[:-1]
        return np.ascontiguousarray(
            np.moveaxis(a.reshape(*lead, H // 2, 2, DH), -3, -1).reshape(*lead, D))

    def rows_by_dim(a):
        return np.ascontiguousarray(np.asarray(a).reshape(H, DH, D).transpose(1, 0, 2).reshape(D, D))

    pos = np.arange(S, dtype=np.float32)[:, None]
    div = np.exp(np.arange(0, D, 2, dtype=np.float32) * np.float32(-np.log(10000.0) / D)).astype(np.float32)
    ang = (pos * div).astype(np.float32)
    pe = np.stack([np.sin(ang), np.cos(ang)], axis=-1).reshape(S, D).astype(np.float32)

    head_of = np.ascontiguousarray(np.broadcast_to(
        np.eye(H, dtype=np.float32).reshape(2, 1, H // 2, H), (2, DH, H // 2, H)).reshape(D, H))

    g = {k[3:]: np.asarray(v) for k, v in inputs.items()}
    def every(a):
        return np.broadcast_to(np.asarray(a).reshape(1, -1), (D, np.asarray(a).size))

    vectors = [g["attn_ln_g"], g["attn_ln_b"], perm(g["attn_bq"]), perm(g["attn_bk"]),
               perm(g["attn_u_bias"].reshape(D)), perm(g["attn_v_bias"].reshape(D)), g["attn_bo"]]
    consts = np.concatenate(
        [np.eye(D, dtype=np.float32), head_of] + [v.reshape(D, 1) for v in vectors]
        + [every(g["ffn_s0"]), every(g["ffn_s1"]), every(g["ffn_s2"]), every(g["attn_bv"]),
           perm(g["attn_Wq"]), perm(g["attn_Wk"]), g["attn_Wv"], rows_by_dim(g["attn_Wo"])], axis=1)
    data = {
        "x": g["attn_x"], "consts": consts, "wp": perm(g["attn_Wp"]), "pe_t": np.ascontiguousarray(pe.T),
        "k0": g["ffn_k0"], "k1": g["ffn_k1"], "k2": g["ffn_k2"],
    }
    nc = bacc.Bacc("TRN2", target_bir_lowering=False, num_devices=1)
    arrays, args = {}, []
    for name, a in data.items():
        a = np.ascontiguousarray(a)
        arrays[f"in_{name}"] = a
        args.append(nc.dram_tensor(f"in_{name}", a.shape, mybir.dt.from_np(a.dtype), kind="ExternalInput").ap())
    out = nc.dram_tensor("out", g["attn_x"].shape, F32, kind="ExternalOutput").ap()
    attention_mlp(nc, *args, out)
    r = run_bass_kernel_spmd(nc, [arrays], core_ids=[0])
    return r.results[0]["out"]
```
